# Optimizing a Trainium2 kernel written in Bass

```python
import numpy as np
import jax
import jax.numpy as jnp

def _softmax(x, axis=-1):
    return jax.nn.softmax(x, axis=axis)

def _gelu(x):
    return jax.nn.gelu(x, approximate=True)

def _silu(x):
    return jax.nn.silu(x)

def _sigmoid(x):
    return jax.nn.sigmoid(x)

def _layernorm(x, axis=-1, eps=1e-05):
    m = jnp.mean(x, axis=axis, keepdims=True)
    v = jnp.var(x, axis=axis, keepdims=True)
    return (x - m) / jnp.sqrt(v + eps)

def _scatter_add(tgt, idx, src, axis=0):
    return tgt.at[idx].add(src)

def _segment_sum(src, seg, n):
    return jax.ops.segment_sum(src, seg, n)
kernel_name = 'mk_seq_postln_d2_jaxref_r8_748766'

def setup_inputs(seed: int=0):
    np.random.seed(seed)
    _w = jnp.asarray

    def _L0_attn_setup():
        import jax, jax.numpy as jnp
        import numpy as np
        EMBED_DIM = 128
        NUM_HEADS = 16
        HEAD_DIM = EMBED_DIM // NUM_HEADS
        R_QKV = 32
        R_OUT = 32
        B, T = (4, 256)
        key = jax.random.key(seed)
        k1, k2, k3, k4, k5 = jax.random.split(key, 5)
        s = 0.02
        return {'x': jax.random.normal(k1, (B, T, EMBED_DIM), dtype=jnp.float32), 'W_qkv_v': jax.random.normal(k2, (R_QKV, EMBED_DIM), dtype=jnp.float32) * s, 'W_qkv_u': jax.random.normal(k3, (3 * EMBED_DIM, R_QKV), dtype=jnp.float32) * s, 'W_o_v': jax.random.normal(k4, (R_OUT, EMBED_DIM), dtype=jnp.float32) * s, 'W_o_u': jax.random.normal(k5, (EMBED_DIM, R_OUT), dtype=jnp.float32) * s}
    _L0_attn_in = _L0_attn_setup()

    def _L0_ffn_setup():
        import jax, jax.numpy as jnp
        import numpy as np
        B, S, H, F, E = (8, 256, 128, 512, 8)
        INIT_LAMBDA = 0.2
        key = jax.random.key(seed)
        ks = jax.random.split(key, 12)
        std = 0.02
        return {'hidden_states': jax.random.normal(ks[0], (B, S, H), jnp.float32), 'gate_w1': jax.random.normal(ks[1], (H, H), jnp.float32) * 0.01, 'gate_b1': jnp.zeros((H,), jnp.float32), 'gate_w2': jax.random.normal(ks[2], (E, H), jnp.float32) * 0.01, 'gate_b2': jnp.full((E,), INIT_LAMBDA, jnp.float32), 'W1': jax.random.normal(ks[3], (F, H), jnp.float32) * std, 'b1': jax.random.normal(ks[4], (F,), jnp.float32) * std, 'W2': jax.random.normal(ks[5], (H, F), jnp.float32) * std, 'b2': jax.random.normal(ks[6], (H,), jnp.float32) * std, 'TW1': jax.random.normal(ks[7], (E, F, H), jnp.float32) * std, 'Tb1': jax.random.normal(ks[8], (E, F), jnp.float32) * std, 'TW2': jax.random.normal(ks[9], (E, H, F), jnp.float32) * std, 'Tb2': jax.random.normal(ks[10], (E, H), jnp.float32) * std}
    _L0_ffn_in = _L0_ffn_setup()

    def _L1_attn_setup():
        import jax, jax.numpy as jnp
        import numpy as np
        B, S, D_MODEL, H = (4, 256, 128, 16)
        HD = D_MODEL // H
        key = jax.random.key(seed)
        k1, k2, k3, k4 = jax.random.split(key, 4)
        x = jax.random.normal(k1, (B, S, D_MODEL), dtype=jnp.float32)
        scale = 1.0 / np.sqrt(D_MODEL)
        Wq = jax.random.normal(k2, (D_MODEL, D_MODEL), dtype=jnp.float32) * scale
        Wk = jax.random.normal(k3, (D_MODEL, D_MODEL), dtype=jnp.float32) * scale
        Wv = jax.random.normal(k4, (D_MODEL, D_MODEL), dtype=jnp.float32) * scale
        return {'x': x, 'Wq': Wq, 'Wk': Wk, 'Wv': Wv}
    _L1_attn_in = _L1_attn_setup()

    def _L1_ffn_setup():
        import jax, jax.numpy as jnp
        import numpy as np
        DIM = 128
        DEPTH = 6
        HEADS = 16
        DIM_HEAD = 64
        WINDOW = 32
        INNER = HEADS * DIM_HEAD
        DIM_INNER = int(DIM * 4 * 2 / 3)
        QK_SCALE = 8.0

        def shift_tokens(t):
            a, s = jnp.split(t, 2, -1)
            s = jnp.pad(s, ((0, 0), (1, 0), (0, 0)))[:, :-1]
            return jnp.concatenate([a, s], -1)

        def l2norm(t):
            return t / jnp.maximum(jnp.linalg.norm(t, axis=-1, keepdims=True), 1e-12)

        def rotate_half(x):
            x1, x2 = jnp.split(x, 2, -1)
            return jnp.concatenate([-x2, x1], -1)

        def rotary_tables(n):
            half = jnp.arange(0, DIM_HEAD, 2, dtype=jnp.float32)
            inv_freq = 1.0 / 10000.0 ** (half / DIM_HEAD)
            t = jnp.arange(n, dtype=jnp.float32)
            freqs = t[:, None] * inv_freq[None, :]
            freqs = jnp.concatenate([freqs, freqs], -1)
            base_scale = (half + 0.4 * DIM_HEAD) / (1.4 * DIM_HEAD)
            power = (t - n // 2) / (WINDOW // 2)
            scale = base_scale[None, :] ** power[:, None]
            scale = jnp.concatenate([scale, scale], -1)
            return (freqs, scale)

        def local_attention(q, k, v):
            b, h, n, d = q.shape
            w = WINDOW
            nw = n // w
            bq = q.reshape(b, h, nw, w, d)
            bk = k.reshape(b, h, nw, w, d)
            bv = v.reshape(b, h, nw, w, d)

            def look(t):
                p = jnp.pad(t, ((0, 0), (0, 0), (1, 0), (0, 0), (0, 0)))
                return jnp.concatenate([p[:, :, :nw], p[:, :, 1:]], axis=3)
            bk2, bv2 = (look(bk), look(bv))
            seq = jnp.arange(n).reshape(nw, w)
            seq_p = jnp.pad(seq, ((1, 0), (0, 0)), constant_values=-1)
            jt = jnp.concatenate([seq_p[:nw], seq_p[1:]], axis=1)
            it = seq[:, :, None]
            jb = jt[:, None, :]
            mask = (it < jb) | (it > jb + w) | (jb == -1)
            sim = jnp.einsum('bhwie,bhwje->bhwij', bq, bk2) * QK_SCALE
            sim = jnp.where(mask, -jnp.finfo(sim.dtype).max, sim)
            attn = jax.nn.softmax(sim, -1)
            out = jnp.einsum('bhwij,bhwje->bhwie', attn, bv2)
            return out.reshape(b, h, n, d)

        def attn_layer(x, Wqkv, qs, ksc, Wo):
            b, n, _ = x.shape
            qkv = x @ Wqkv
            q, k, v = jnp.split(qkv, 3, -1)
            sh = lambda t: t.reshape(b, n, HEADS, DIM_HEAD).transpose(0, 2, 1, 3)
            q, k, v = (sh(q), sh(k), sh(v))
            q = l2norm(q) * qs
            k = l2norm(k) * ksc
            freqs, scale = rotary_tables(n)
            cos, sin = (jnp.cos(freqs), jnp.sin(freqs))
            q = q * cos * scale + rotate_half(q) * sin * scale
            inv = 1.0 / scale
            k = k * cos * inv + rotate_half(k) * sin * inv
            out = local_attention(q, k, v)
            out = out.transpose(0, 2, 1, 3).reshape(b, n, INNER)
            return out @ Wo

        def ffn_layer(x, g, bln, W1, b1, W2, b2):
            mu = x.mean(-1, keepdims=True)
            var = ((x - mu) ** 2).mean(-1, keepdims=True)
            xn = (x - mu) / jnp.sqrt(var + 1e-05) * g + bln
            hg = xn @ W1 + b1
            a, gate = jnp.split(hg, 2, -1)
            return a * jax.nn.gelu(gate, approximate=False) @ W2 + b2
        key = jax.random.key(seed)
        ks = jax.random.split(key, 8)
        B, N = (2, 256)
        init = lambda k, shape: jax.random.normal(k, shape, jnp.float32) * 0.02
        return {'x': jax.random.normal(ks[0], (B, N, DIM), jnp.float32), 'Wqkv': init(ks[1], (DEPTH, DIM, 3 * INNER)), 'q_scale': jnp.ones((DEPTH, DIM_HEAD), jnp.float32), 'k_scale': jnp.ones((DEPTH, DIM_HEAD), jnp.float32), 'Wo': init(ks[2], (DEPTH, INNER, DIM)), 'ln_g': jnp.ones((DEPTH, DIM), jnp.float32), 'ln_b': jnp.zeros((DEPTH, DIM), jnp.float32), 'W1': init(ks[3], (DEPTH, DIM, 2 * DIM_INNER)), 'b1': jnp.zeros((DEPTH, 2 * DIM_INNER), jnp.float32), 'W2': init(ks[4], (DEPTH, DIM_INNER, DIM)), 'b2': jnp.zeros((DEPTH, DIM), jnp.float32)}
    _L1_ffn_in = _L1_ffn_setup()
    _d = {'L0_attn_x': _L0_attn_in['x'], 'L0_attn_W_qkv_v': _L0_attn_in['W_qkv_v'], 'L0_attn_W_qkv_u': _L0_attn_in['W_qkv_u'], 'L0_attn_W_o_v': _L0_attn_in['W_o_v'], 'L0_attn_W_o_u': _L0_attn_in['W_o_u'], 'L0_ffn_gate_w1': _L0_ffn_in['gate_w1'], 'L0_ffn_gate_b1': _L0_ffn_in['gate_b1'], 'L0_ffn_gate_w2': _L0_ffn_in['gate_w2'], 'L0_ffn_gate_b2': _L0_ffn_in['gate_b2'], 'L0_ffn_W1': _L0_ffn_in['W1'], 'L0_ffn_b1': _L0_ffn_in['b1'], 'L0_ffn_W2': _L0_ffn_in['W2'], 'L0_ffn_b2': _L0_ffn_in['b2'], 'L0_ffn_TW1': _L0_ffn_in['TW1'], 'L0_ffn_Tb1': _L0_ffn_in['Tb1'], 'L0_ffn_TW2': _L0_ffn_in['TW2'], 'L0_ffn_Tb2': _L0_ffn_in['Tb2'], 'L1_attn_Wq': _L1_attn_in['Wq'], 'L1_attn_Wk': _L1_attn_in['Wk'], 'L1_attn_Wv': _L1_attn_in['Wv'], 'L1_ffn_Wqkv': _L1_ffn_in['Wqkv'], 'L1_ffn_q_scale': _L1_ffn_in['q_scale'], 'L1_ffn_k_scale': _L1_ffn_in['k_scale'], 'L1_ffn_Wo': _L1_ffn_in['Wo'], 'L1_ffn_ln_g': _L1_ffn_in['ln_g'], 'L1_ffn_ln_b': _L1_ffn_in['ln_b'], 'L1_ffn_W1': _L1_ffn_in['W1'], 'L1_ffn_b1': _L1_ffn_in['b1'], 'L1_ffn_W2': _L1_ffn_in['W2'], 'L1_ffn_b2': _L1_ffn_in['b2']}
    _x0 = _d['L0_attn_x']
    _d['L0_attn_x'] = jax.random.normal(jax.random.fold_in(jax.random.key(seed), 1), (4, 1024, 128), dtype=_x0.dtype)
    del _x0
    return _d

def reference(L0_attn_x, L0_attn_W_qkv_v, L0_attn_W_qkv_u, L0_attn_W_o_v, L0_attn_W_o_u, L0_ffn_gate_w1, L0_ffn_gate_b1, L0_ffn_gate_w2, L0_ffn_gate_b2, L0_ffn_W1, L0_ffn_b1, L0_ffn_W2, L0_ffn_b2, L0_ffn_TW1, L0_ffn_Tb1, L0_ffn_TW2, L0_ffn_Tb2, L1_attn_Wq, L1_attn_Wk, L1_attn_Wv, L1_ffn_Wqkv, L1_ffn_q_scale, L1_ffn_k_scale, L1_ffn_Wo, L1_ffn_ln_g, L1_ffn_ln_b, L1_ffn_W1, L1_ffn_b1, L1_ffn_W2, L1_ffn_b2):

    def _L0_attn_ref(x, W_qkv_v, W_qkv_u, W_o_v, W_o_u):
        import jax, jax.numpy as jnp
        import numpy as np
        EMBED_DIM = 128
        NUM_HEADS = 16
        HEAD_DIM = EMBED_DIM // NUM_HEADS
        R_QKV = 32
        R_OUT = 32
        B, T = (4, 256)
        Bq, Tq, C = x.shape
        H, D = (NUM_HEADS, HEAD_DIM)
        qkv = x @ W_qkv_v.T @ W_qkv_u.T
        q, k, v = jnp.split(qkv, 3, axis=-1)
        q = q.reshape(Bq, Tq, H, D).transpose(0, 2, 1, 3)
        k = k.reshape(Bq, Tq, H, D).transpose(0, 2, 1, 3)
        v = v.reshape(Bq, Tq, H, D).transpose(0, 2, 1, 3)
        scale = 1.0 / jnp.sqrt(jnp.asarray(D, dtype=x.dtype))
        scores = jnp.einsum('bhtd,bhsd->bhts', q, k) * scale
        attn = jax.nn.softmax(scores.astype(jnp.float32), axis=-1).astype(q.dtype)
        y = jnp.einsum('bhts,bhsd->bhtd', attn, v)
        y = y.transpose(0, 2, 1, 3).reshape(Bq, Tq, C)
        y = y @ W_o_v.T @ W_o_u.T
        return y

    def _L0_ffn_ref(hidden_states, gate_w1, gate_b1, gate_w2, gate_b2, W1, b1, W2, b2, TW1, Tb1, TW2, Tb2):
        import jax, jax.numpy as jnp
        import numpy as np
        B, S, H, F, E = (8, 256, 128, 512, 8)
        INIT_LAMBDA = 0.2
        x = hidden_states
        h = jax.nn.relu(jnp.einsum('bsh,oh->bso', x, gate_w1) + gate_b1)
        g = jnp.einsum('bso,eo->bse', h, gate_w2) + gate_b2
        g = g.mean(axis=1)
        mW1 = W1 + jnp.einsum('be,efh->bfh', g, TW1)
        mb1 = b1 + g @ Tb1
        mW2 = W2 + jnp.einsum('be,ehf->bhf', g, TW2)
        mb2 = b2 + g @ Tb2
        u = jax.nn.gelu(jnp.einsum('bsh,bfh->bsf', x, mW1) + mb1[:, None, :])
        out = jnp.einsum('bsf,bhf->bsh', u, mW2) + mb2[:, None, :]
        return out

    def _L1_attn_ref(x, Wq, Wk, Wv):
        import jax, jax.numpy as jnp
        import numpy as np
        B, S, D_MODEL, H = (4, 256, 128, 16)
        HD = D_MODEL // H
        b, s, d_in = x.shape
        h, hd = (H, HD)
        q = (x @ Wq).reshape(b, s, h, hd).transpose(0, 2, 1, 3)
        k = (x @ Wk).reshape(b, s, h, hd).transpose(0, 2, 1, 3)
        v = (x @ Wv).reshape(b, s, h, hd).transpose(0, 2, 1, 3)
        scores = jnp.einsum('bhqd,bhkd->bhqk', q, k)
        causal = jnp.tril(jnp.ones((s, s), dtype=bool))
        scores = jnp.where(causal, scores, -jnp.inf)
        attn = jax.nn.softmax(scores / jnp.sqrt(jnp.float32(hd)), axis=-1)
        ctx = jnp.einsum('bhqk,bhkd->bhqd', attn, v)
        return ctx.transpose(0, 2, 1, 3).reshape(b, s, h * hd)

    def _L1_ffn_ref(x, Wqkv, q_scale, k_scale, Wo, ln_g, ln_b, W1, b1, W2, b2):
        import jax, jax.numpy as jnp
        import numpy as np
        DIM = 128
        DEPTH = 6
        HEADS = 16
        DIM_HEAD = 64
        WINDOW = 32
        INNER = HEADS * DIM_HEAD
        DIM_INNER = int(DIM * 4 * 2 / 3)
        QK_SCALE = 8.0

        def shift_tokens(t):
            a, s = jnp.split(t, 2, -1)
            s = jnp.pad(s, ((0, 0), (1, 0), (0, 0)))[:, :-1]
            return jnp.concatenate([a, s], -1)

        def l2norm(t):
            return t / jnp.maximum(jnp.linalg.norm(t, axis=-1, keepdims=True), 1e-12)

        def rotate_half(x):
            x1, x2 = jnp.split(x, 2, -1)
            return jnp.concatenate([-x2, x1], -1)

        def rotary_tables(n):
            half = jnp.arange(0, DIM_HEAD, 2, dtype=jnp.float32)
            inv_freq = 1.0 / 10000.0 ** (half / DIM_HEAD)
            t = jnp.arange(n, dtype=jnp.float32)
            freqs = t[:, None] * inv_freq[None, :]
            freqs = jnp.concatenate([freqs, freqs], -1)
            base_scale = (half + 0.4 * DIM_HEAD) / (1.4 * DIM_HEAD)
            power = (t - n // 2) / (WINDOW // 2)
            scale = base_scale[None, :] ** power[:, None]
            scale = jnp.concatenate([scale, scale], -1)
            return (freqs, scale)

        def local_attention(q, k, v):
            b, h, n, d = q.shape
            w = WINDOW
            nw = n // w
            bq = q.reshape(b, h, nw, w, d)
            bk = k.reshape(b, h, nw, w, d)
            bv = v.reshape(b, h, nw, w, d)

            def look(t):
                p = jnp.pad(t, ((0, 0), (0, 0), (1, 0), (0, 0), (0, 0)))
                return jnp.concatenate([p[:, :, :nw], p[:, :, 1:]], axis=3)
            bk2, bv2 = (look(bk), look(bv))
            seq = jnp.arange(n).reshape(nw, w)
            seq_p = jnp.pad(seq, ((1, 0), (0, 0)), constant_values=-1)
            jt = jnp.concatenate([seq_p[:nw], seq_p[1:]], axis=1)
            it = seq[:, :, None]
            jb = jt[:, None, :]
            mask = (it < jb) | (it > jb + w) | (jb == -1)
            sim = jnp.einsum('bhwie,bhwje->bhwij', bq, bk2) * QK_SCALE
            sim = jnp.where(mask, -jnp.finfo(sim.dtype).max, sim)
            attn = jax.nn.softmax(sim, -1)
            out = jnp.einsum('bhwij,bhwje->bhwie', attn, bv2)
            return out.reshape(b, h, n, d)

        def attn_layer(x, Wqkv, qs, ksc, Wo):
            b, n, _ = x.shape
            qkv = x @ Wqkv
            q, k, v = jnp.split(qkv, 3, -1)
            sh = lambda t: t.reshape(b, n, HEADS, DIM_HEAD).transpose(0, 2, 1, 3)
            q, k, v = (sh(q), sh(k), sh(v))
            q = l2norm(q) * qs
            k = l2norm(k) * ksc
            freqs, scale = rotary_tables(n)
            cos, sin = (jnp.cos(freqs), jnp.sin(freqs))
            q = q * cos * scale + rotate_half(q) * sin * scale
            inv = 1.0 / scale
            k = k * cos * inv + rotate_half(k) * sin * inv
            out = local_attention(q, k, v)
            out = out.transpose(0, 2, 1, 3).reshape(b, n, INNER)
            return out @ Wo

        def ffn_layer(x, g, bln, W1, b1, W2, b2):
            mu = x.mean(-1, keepdims=True)
            var = ((x - mu) ** 2).mean(-1, keepdims=True)
            xn = (x - mu) / jnp.sqrt(var + 1e-05) * g + bln
            hg = xn @ W1 + b1
            a, gate = jnp.split(hg, 2, -1)
            return a * jax.nn.gelu(gate, approximate=False) @ W2 + b2
        for i in range(DEPTH):
            x = attn_layer(shift_tokens(x), Wqkv[i], q_scale[i], k_scale[i], Wo[i]) + x
            x = ffn_layer(shift_tokens(x), ln_g[i], ln_b[i], W1[i], b1[i], W2[i], b2[i]) + x
        return x
    x = L0_attn_x
    x = _layernorm(x + _L0_attn_ref(x, L0_attn_W_qkv_v, L0_attn_W_qkv_u, L0_attn_W_o_v, L0_attn_W_o_u), axis=-1)
    x = _layernorm(x + _L0_ffn_ref(x, L0_ffn_gate_w1, L0_ffn_gate_b1, L0_ffn_gate_w2, L0_ffn_gate_b2, L0_ffn_W1, L0_ffn_b1, L0_ffn_W2, L0_ffn_b2, L0_ffn_TW1, L0_ffn_Tb1, L0_ffn_TW2, L0_ffn_Tb2), axis=-1)
    x = _layernorm(x + _L1_attn_ref(x, L1_attn_Wq, L1_attn_Wk, L1_attn_Wv), axis=-1)
    x = _layernorm(x + _L1_ffn_ref(x, L1_ffn_Wqkv, L1_ffn_q_scale, L1_ffn_k_scale, L1_ffn_Wo, L1_ffn_ln_g, L1_ffn_ln_b, L1_ffn_W1, L1_ffn_b1, L1_ffn_W2, L1_ffn_b2), axis=-1)
    return x

_drawn_inputs = setup_inputs


def setup_inputs(seed=0):
    import zlib

    import numpy as np

    out = dict(_drawn_inputs(seed))
    spreads = {'L0_ffn_gate_b1': (0.0, 0.8),
     'L0_ffn_gate_b2': (0.20000000298023224, 0.6),
     'L1_ffn_q_scale': (1.0, 0.6),
     'L1_ffn_k_scale': (1.0, 0.6),
     'L1_ffn_ln_g': (1.0, 0.6),
     'L1_ffn_ln_b': (0.0, 0.8),
     'L1_ffn_b1': (0.0, 0.8),
     'L1_ffn_b2': (0.0, 0.1)}
    factors = {'L0_attn_W_qkv_v': 8.0,
     'L0_attn_W_qkv_u': 8.0,
     'L0_attn_W_o_v': 8.0,
     'L0_attn_W_o_u': 8.0,
     'L0_ffn_gate_w1': 8.0,
     'L0_ffn_gate_w2': 8.0,
     'L0_ffn_b1': 7.411,
     'L0_ffn_Tb1': 8.0,
     'L0_ffn_Tb2': 4.154,
     'L1_ffn_W1': 3.679,
     'L1_ffn_W2': 3.621}
    for name, (base, spread) in spreads.items():
        noise = np.random.default_rng([zlib.crc32(name.encode()), seed]).standard_normal(out[name].shape)
        drawn = base * np.exp(spread * noise) if base else spread * noise
        out[name] = jnp.asarray(drawn.astype(out[name].dtype))
    for name, factor in factors.items():
        out[name] = (out[name] * factor).astype(out[name].dtype)
    return out
```

```python
from contextlib import ExitStack

import concourse.bass as bass
import numpy as np
from concourse import mybir

F32 = mybir.dt.float32
BF16 = mybir.dt.bfloat16
ALU = mybir.AluOpType
ACT = mybir.ActivationFunctionType
AX_X = mybir.AxisListType.X

P = 128
BATCH, SEQ, DIM = 4, 1024, 128
TOKENS = BATCH * SEQ
TILES = TOKENS // P
TPB = SEQ // P
CH = 512
CHUNKS = TOKENS // CH
HEADS = 16
HD = DIM // HEADS
RANK = 32
FF, EXPERTS = 512, 8
DEPTH, DH, WIN = 6, 64, 32
INNER = HEADS * DH
DI = int(DIM * 4 * 2 / 3)
EPS = 1e-5
PADL = 2
SLOTS = PADL + TILES + PADL
NEG = -3.0e38
PARTS = 6
Q_PART = (0, 0, 1, 1, 0, 2)
K_PART = (0, 1, 0, 1, 2, 0)
KROWS = PARTS * HD
GH = 4
GROUPS = BATCH * HEADS // GH
SM_SCALE = 1.0 / float(np.sqrt(np.float32(HD)))


FIRST = 1


def ds(start, n):
    return bass.ds(start, n)


def semaphores(nc, ctx, tag):
    taken = []

    def clear():
        nc.clear_and_free_semaphores(taken)
        nc.all_engine_barrier()

    def sem(name, start=FIRST):
        taken.append(nc.alloc_semaphore(f"{tag}_{name}"))
        if start:
            nc.sync.sem_inc(taken[-1], start)
        return taken[-1]

    ctx.callback(clear)
    return sem


def layer_norm_pe(nc, pe, stat, ones, resid, sq, ln, n):
    pe.wait_ge(ln["resid"], n + 1 + FIRST)
    nc.tensor.matmul(stat[:, 0, :], ones[:, :], resid[:, :], start=True, stop=True).then_inc(ln["mean"], 1)
    pe.wait_ge(ln["sq"], n + 1 + FIRST)
    nc.tensor.matmul(stat[:, 1, :], ones[:, :], sq[:, :], start=True, stop=True).then_inc(ln["var"], 1)


def layer_norm_act(nc, act, stat, sd, eps, ln, n):
    act.wait_ge(ln["var"], n + 1 + FIRST)
    act.wait_ge(ln["inv"], n + FIRST)
    nc.scalar.activation(sd[:, :], stat[:, 1, :], ACT.Sqrt, bias=eps[:, 0:1]).then_inc(ln["sd"], 1)


def layer_norm_dve(nc, dve, stat, resid, sq, sd, out, ln, n, extra=None):
    dve.wait_ge(ln["mean"], n + 1 + FIRST)
    nc.vector.tensor_tensor(resid[:, :], resid[:, :], stat[:, 0, :], ALU.subtract).then_inc(ln["cent"], 1)
    dve.wait_ge(ln["cent"], n + 1 + FIRST)
    nc.vector.tensor_tensor(sq[:, :], resid[:, :], resid[:, :], ALU.mult).then_inc(ln["sq"], 1)
    dve.wait_ge(ln["sd"], n + 1 + FIRST)
    nc.vector.reciprocal(sd[:, :], sd[:, :]).then_inc(ln["inv"], 1)
    dve.wait_ge(ln["inv"], n + 1 + FIRST)
    nc.vector.tensor_tensor(out, resid[:, :], sd[:, :], ALU.mult).then_inc(ln["out"], 1)
    if extra is not None:
        dve.wait_ge(ln["out"], n + 1 + FIRST)
        nc.vector.tensor_copy(extra, out).then_inc(ln["kept"], 1)


def build(nc, A, out_dram):
    with ExitStack() as whole:
        def keep(name, shape, dt=F32):
            return whole.enter_context(nc.sbuf_tensor(name, shape, dt))

        XT = keep("XT", [P, SLOTS * P])
        X0 = PADL * P
        xin = keep("xin", [P, TOKENS])
        ident = keep("ident", [P, P])
        ones = keep("ones", [P, P])
        eps = keep("eps", [P, 1])
        q_parts = nc.dram_tensor("q_parts", [BATCH * P, PARTS, SEQ], BF16, kind="Internal").ap()
        k_parts = nc.dram_tensor("k_parts", [BATCH * P, PARTS, SEQ], BF16, kind="Internal").ap()

        with ExitStack() as ctx:
            loaded = semaphores(nc, ctx, "s0")("loaded", 0)
            with nc.Block() as block:
                @block.sync
                def _(sp):
                    sp.dma_start(XT[:, X0:X0 + TOKENS], A["x"]).then_inc(loaded, 16)
                    sp.dma_start(ident[:, :], A["c_ident"]).then_inc(loaded, 16)
                    sp.wait_ge(loaded, 32)

                @block.vector
                def _(dve):
                    nc.vector.memset(ones[:, :], 1.0 / DIM)
                    nc.vector.memset(eps[:, :], EPS)
                    nc.vector.memset(XT[:, 0:X0], 0.0)
                    nc.vector.memset(XT[:, X0 + TOKENS:SLOTS * P], 0.0)

        with ExitStack() as ctx:
            vals = ctx.enter_context(nc.sbuf_tensor("a1_vals", [P, TILES, HEADS, HD + 1], F32))
            attn = ctx.enter_context(nc.sbuf_tensor("a1_attn", [P, TILES, DIM], F32))
            project(nc, A, "a1", XT, X0, vals, q_parts, k_parts, low_rank=True)
            attention(nc, A, "a1", vals, attn, q_parts, k_parts, ident, causal=False)
            finish(nc, A, "a1", XT, X0, attn, ident, ones, eps, None, low_rank=True)
        expert_ffn(nc, A, XT, X0, ones, eps)
        with ExitStack() as ctx:
            vals = ctx.enter_context(nc.sbuf_tensor("a2_vals", [P, TILES, HEADS, HD + 1], F32))
            attn = ctx.enter_context(nc.sbuf_tensor("a2_attn", [P, TILES, DIM], F32))
            project(nc, A, "a2", XT, X0, vals, q_parts, k_parts, low_rank=False)
            attention(nc, A, "a2", vals, attn, q_parts, k_parts, ident, causal=True)
            finish(nc, A, "a2", XT, X0, attn, ident, ones, eps, xin, low_rank=False)
        windowed(nc, A, XT, ident, ones, eps)
        last_norm(nc, XT, X0, xin, ones, eps, out_dram)


def project(nc, A, tag, XT, X0, vals, q_parts, k_parts, low_rank):
    with ExitStack() as ctx:
        def sb(name, shape, dt=F32):
            return ctx.enter_context(nc.sbuf_tensor(f"{tag}p_{name}", shape, dt))

        sem = semaphores(nc, ctx, f"{tag}p")

        KD = RANK if low_rank else DIM
        wdown = sb("wdown", [DIM, RANK])
        w = sb("w", [KD, 3 * DIM])
        src = sb("src", [KD, CH])
        part = sb("part", [P, 2, 3, CH], BF16)
        rest = sb("rest", [P, 2, 2, CH])
        p_src = ctx.enter_context(nc.psum_tensor(f"{tag}p_psrc", [P, CH], F32))
        p_qk = ctx.enter_context(nc.psum_tensor(f"{tag}p_pqk", [P, 2, CH], F32))
        p_v = ctx.enter_context(nc.psum_tensor(f"{tag}p_pv", [P, 4, DIM], F32))
        weights, down, src_ready = sem("weights", 0), sem("down"), sem("src_ready")
        projected, first, rest1 = sem("projected"), sem("first"), sem("rest1")
        second, third, v_ready, v_kept = sem("second"), sem("third"), sem("v_ready"), sem("v_kept")
        stored = [sem("q_stored", 0), sem("k_stored", 0)]
        with nc.Block() as block:
            @block.sync
            def _(sp):
                if low_rank:
                    sp.dma_start(wdown[:, :], A["qkv_down"]).then_inc(weights, 16)
                    sp.dma_start(w[:, :], A["qkv_up"]).then_inc(weights, 16)
                else:
                    sp.dma_start(w[:, 0:DIM], A["wq"]).then_inc(weights, 16)
                    sp.dma_start(w[:, DIM:2 * DIM], A["wk"]).then_inc(weights, 16)
                    sp.dma_start(w[:, 2 * DIM:3 * DIM], A["wv"]).then_inc(weights, 16)
                for c in range(CHUNKS):
                    b, col = c // 2, c % 2 * CH
                    for s, (order, dst) in enumerate(((Q_PART, q_parts), (K_PART, k_parts))):
                        sp.wait_ge(third, 2 * c + s + 1 + FIRST)
                        for g, j in enumerate(order):
                            sp.dma_start(dst[b * P:(b + 1) * P, g, col:col + CH],
                                         part[:, s, j, :]).then_inc(stored[s], 16)
                for s in range(2):
                    sp.wait_ge(stored[s], CHUNKS * PARTS * 16)

            @block.tensor
            def _(pe):
                pe.wait_ge(weights, 32 if low_rank else 48)
                with pe.Fori(0, CHUNKS) as c:
                    if low_rank:
                        pe.wait_ge(src_ready, c + FIRST)
                        nc.tensor.matmul(p_src[0:RANK, :], wdown[:, :], XT[:, ds(c * CH + X0, CH)],
                                         start=True, stop=True).then_inc(down, 1)
                    pe.wait_ge(src_ready, c + 1 + FIRST)
                    pe.wait_ge(third, 2 * c + FIRST)
                    for s in range(2):
                        nc.tensor.matmul(p_qk[:, s, :], w[:, s * DIM:(s + 1) * DIM], src[:, :],
                                         start=True, stop=True).then_inc(projected, 1)
                    pe.wait_ge(v_kept, c + FIRST)
                    for t in range(4):
                        mm = nc.tensor.matmul(p_v[:, t, :], src[:, t * P:(t + 1) * P],
                                              w[:, 2 * DIM:3 * DIM], start=True, stop=True)
                    mm.then_inc(v_ready, 1)

            @block.scalar
            def _(act):
                with act.Fori(0, CHUNKS) as c:
                    if low_rank:
                        act.wait_ge(down, c + 1 + FIRST)
                        act.wait_ge(v_ready, c + FIRST)
                        nc.scalar.copy(src[:, :], p_src[0:RANK, :]).then_inc(src_ready, 1)
                    else:
                        act.wait_ge(v_ready, c + FIRST)
                        nc.scalar.copy(src[:, :], XT[:, ds(c * CH + X0, CH)]).then_inc(src_ready, 1)
                    act.wait_ge(v_ready, c + 1 + FIRST)
                    nc.scalar.copy(vals[:, ds(c * 4, 4), :, 0:HD],
                                   p_v[:, :, :].rearrange("p t (h d) -> p t h d", h=HEADS)).then_inc(v_kept, 1)

            @block.vector
            def _(dve):
                ones_col = vals[:, :, :, HD:HD + 1].rearrange("p t h o -> p (t h) o")
                nc.vector.memset(ones_col, 1.0)
                for c in range(CHUNKS):
                    for s in range(2):
                        n = 2 * c + s
                        dve.wait_ge(projected, n + 1 + FIRST)
                        if c:
                            dve.wait_ge(stored[s], c * PARTS * 16)
                        nc.vector.tensor_copy(part[:, s, 0, :], p_qk[:, s, :]).then_inc(first, 1)
                        dve.wait_ge(first, n + 1 + FIRST)
                        nc.vector.tensor_tensor(rest[:, s, 0, :], p_qk[:, s, :], part[:, s, 0, :],
                                                ALU.subtract).then_inc(rest1, 1)
                        dve.wait_ge(rest1, n + 1 + FIRST)
                        nc.vector.tensor_copy(part[:, s, 1, :], rest[:, s, 0, :]).then_inc(second, 1)
                        dve.wait_ge(second, n + 1 + FIRST)
                        nc.vector.tensor_tensor(part[:, s, 2, :], rest[:, s, 0, :], part[:, s, 1, :],
                                                ALU.subtract).then_inc(third, 1)


def attention(nc, A, tag, vals, attn, q_parts, k_parts, ident, causal):
    with ExitStack() as ctx:
        def sb(name, shape, dt=F32):
            return ctx.enter_context(nc.sbuf_tensor(f"{tag}_{name}", shape, dt))

        sem = semaphores(nc, ctx, f"{tag}")

        QS = sb("QS", [P, 2, GH, SEQ], BF16)
        KS = sb("KS", [P, 2, GH, SEQ], BF16)
        KZ = sb("KZ", [P, 2, GH, SEQ], BF16)
        V = [sb(f"V{i}", [P, TPB, GH, 32]) for i in range(2)]
        probs = sb("probs", [P, 2, GH, CH])
        mpart = sb("mpart", [P, GH, TPB, 2])
        mcol = sb("mcol", [P, GH * TPB])
        mrow = sb("mrow", [GH * TPB, 3, P], BF16)
        mrest = sb("mrest", [GH * TPB, P])
        osum = sb("osum", [P, CH])
        rsum = sb("rsum", [P, 4 * GH, 1])
        cmask = sb("cmask", [P, 3, P])
        cmaskb = sb("cmaskb", [P, 3, P], BF16)
        p_s = ctx.enter_context(nc.psum_tensor(f"{tag}_ps", [P, 2, 2, CH], F32))
        p_m = ctx.enter_context(nc.psum_tensor(f"{tag}_pm", [P, 2, CH], F32))
        p_o = ctx.enter_context(nc.psum_tensor(f"{tag}_po", [P, CH], F32))
        p_t = ctx.enter_context(nc.psum_tensor(f"{tag}_pt", [P, 4, GH, 32], F32))

        if causal:
            steps = [(hq, kt, max(0, kt * P - hq * CH)) for hq in range(2) for kt in range(4 * hq + 4)]
            chunks = [(h, qt, kc, min(CH, (qt + 1) * P - kc * CH)) for qt in range(TPB)
                      for h in range(GH) for kc in range(qt * P // CH + 1)]
        else:
            steps = [(hq, kt, 0) for hq in range(2) for kt in range(TPB)]
            chunks = [(h, qt, kc, CH) for qt in range(TPB) for h in range(GH) for kc in range(2)]
        NS, NC = len(steps), len(chunks)
        ends = [s for s in range(NS) if s == NS - 1 or steps[s + 1][0] != steps[s][0]]
        per_step = -(-NC // (NS - 3))

        operands, stage_ready = sem("operands", 0), sem("stage_ready")
        maxima, max_read = sem("maxima"), sem("max_read")
        m_all, m_turned, m_lead, m_left, m_split, m_stored = (
            sem("m_all"), sem("m_turned"), sem("m_lead"), sem("m_left"), sem("m_split"), sem("m_stored", 0))
        scores, exped, weighted = sem("scores"), sem("exped"), sem("weighted")
        o_kept, o_turned, o_inv, o_stored = sem("o_kept"), sem("o_turned"), sem("o_inv"), sem("o_stored")
        v_ready, consts, cast, zeroed = sem("v_ready"), sem("consts", 0), sem("cast"), sem("zeroed")
        m_part2, m_done2 = sem("m_part2"), sem("m_mid")

        with nc.Block() as block:
            @block.sync
            def _(sp):
                sp.dma_start(cmask[:, :, :], A["c_causal"]).then_inc(consts, 16)
                sp.wait_ge(zeroed, 5 + FIRST)
                qg = q_parts.rearrange("(g h d) j t -> g (d j) h t", h=GH, d=HD)
                kg = k_parts.rearrange("(g h d) j t -> g (d j) h t", h=GH, d=HD)

                def load(g, par):
                    for h in range(GH):
                        sp.dma_start(QS[0:KROWS, par, h, :], qg[g, :, h, :]).then_inc(operands, 16)
                        sp.dma_start(KZ[0:KROWS, par, h, :], kg[g, :, h, :]).then_inc(operands, 16)
                        sp.dma_start(KS[0:KROWS, par, h, :], kg[g, :, h, :]).then_inc(operands, 16)

                load(0, 0)
                load(1, 1)
                for g in range(2, GROUPS + 1):
                    sp.wait_ge(scores, 2 * NS * (g - 1) + FIRST)
                    load(g % GROUPS, g % 2)

            @block.gpsimd
            def _(pool):
                nc.gpsimd.memset(KS[:, :, :, :], 0.0).then_inc(zeroed, 1)
                nc.gpsimd.memset(V[0][:, :, :, :], 0.0).then_inc(v_ready, 1)
                nc.gpsimd.memset(V[1][:, :, :, :], 0.0).then_inc(v_ready, 1)
                pool.wait_ge(v_ready, 2 + FIRST)
                with pool.Fori(0, GROUPS // 2) as i:
                    for par in range(2):
                        g = i * 2 + par
                        pool.wait_ge(v_ready, 2 + FIRST)
                        pool.wait_ge(weighted, g * NS + FIRST)
                        src = vals[:, ds(i // 2 * TPB, TPB), ds((i % 2) * 2 * GH + par * GH, GH), :]
                        nc.gpsimd.tensor_copy(V[par][:, :, :, 0:HD + 1], src).then_inc(v_ready, 1)

            @block.vector
            def _(dve):
                nc.vector.memset(QS[:, :, :, :], 0.0).then_inc(zeroed, 1)
                nc.vector.memset(KZ[:, :, :, :], 0.0).then_inc(zeroed, 1)
                nc.vector.memset(mpart[:, :, :, :], NEG).then_inc(zeroed, 1)
                dve.wait_ge(zeroed, 4 + FIRST)
                nc.vector.memset(KS[32:64, :, :, :], -1.0).then_inc(zeroed, 1)
                dve.wait_ge(zeroed, 5 + FIRST)
                dve.wait_ge(consts, 16)
                nc.vector.tensor_copy(cmaskb[:, :, :], cmask[:, :, :]).then_inc(cast, 1)

                def half_max(k, g):
                    h, qt, kc, width = chunks[k]
                    dve.wait_ge(maxima, g * NC + (k + 1) + FIRST)
                    nc.vector.reduce_max(mpart[:, h, qt, kc:kc + 1], p_m[:, k % 2, 0:width],
                                         AX_X).then_inc(max_read, 1)

                def finish_maxima(g):
                    dve.wait_ge(max_read, (g + 1) * NC + FIRST)
                    nc.vector.tensor_reduce(mcol[:, :], mpart[:, :, :, :].rearrange("p h q c -> p (h q) c"),
                                            AX_X, ALU.max).then_inc(m_all, 1)
                    dve.wait_ge(m_turned, g + 1 + FIRST)
                    rows = p_t[0:GH * TPB, :, :, :].rearrange("p a h d -> p (a h d)")[:, 0:P]
                    nc.vector.tensor_copy(mrow[:, 0, :], rows).then_inc(m_lead, 1)
                    dve.wait_ge(m_lead, g + 1 + FIRST)
                    nc.vector.tensor_tensor(mrest[:, :], rows, mrow[:, 0, :], ALU.subtract).then_inc(m_left, 1)
                    dve.wait_ge(m_left, g + 1 + FIRST)
                    nc.vector.tensor_copy(mrow[:, 1, :], mrest[:, :]).then_inc(m_part2, 1)
                    dve.wait_ge(m_part2, g + 1 + FIRST)
                    nc.vector.tensor_tensor(mrow[:, 2, :], mrest[:, :], mrow[:, 1, :],
                                            ALU.subtract).then_inc(m_split, 1)

                def keep_out(g, half):
                    u = g * 2 + half
                    dve.wait_ge(weighted, g * NS + ends[half] + 1 + FIRST)
                    dve.wait_ge(o_turned, u + FIRST)
                    nc.vector.tensor_copy(osum[:, :], p_o[:, :]).then_inc(o_kept, 1)

                def normalise(g, half, pos):
                    u = g * 2 + half
                    dve.wait_ge(o_turned, u + 1 + FIRST)
                    nc.vector.reciprocal(rsum[:, :, :],
                                         p_t[:, :, :, HD:HD + 1].rearrange("p a h o -> p (a h) o")).then_inc(o_inv, 1)
                    dve.wait_ge(o_inv, u + 1 + FIRST)
                    tile, head = pos
                    dst = attn[:, ds(tile + 4 * half, 4), ds(head * HD, GH * HD)]
                    nc.vector.tensor_tensor(
                        dst.rearrange("p a (h d) -> p a h d", h=GH),
                        p_t[:, :, :, 0:HD],
                        rsum[:, :, :].rearrange("p (a h) o -> p a h o", a=4).broadcast_to([P, 4, GH, HD]),
                        ALU.mult).then_inc(o_stored, 1)

                for k in range(NC):
                    half_max(k, 0)
                finish_maxima(0)
                with dve.Fori(0, GROUPS // 2) as i:
                    for par in range(2):
                        g = i * 2 + par
                        pos = (i // 2 * TPB, (i % 2) * 2 * GH + par * GH)
                        k = 0
                        for s in range(NS):
                            if s == ends[0] + 2:
                                keep_out(g, 0)
                            while k < min(NC, (s + 1) * per_step):
                                half_max(k, g + 1)
                                k += 1
                            if s == ends[0] + 2:
                                normalise(g, 0, pos)
                            if s == NS - 3:
                                finish_maxima(g + 1)
                        keep_out(g, 1)
                        normalise(g, 1, pos)

            @block.tensor
            def _(pe):
                pe.wait_ge(cast, 1 + FIRST)

                def max_chunk(k, g, par):
                    h, qt, kc, width = chunks[k]
                    if g is not None:
                        pe.wait_ge(max_read, g * NC + k - 1 + FIRST)
                    elif k >= 2:
                        pe.wait_ge(max_read, k - 1 + FIRST)
                    diag = causal and kc * CH + width == (qt + 1) * P
                    out = p_m[:, k % 2, 0:width]
                    mm = nc.tensor.matmul(out, QS[:, par, h, qt * P:(qt + 1) * P],
                                          KZ[:, par, h, kc * CH:kc * CH + width], start=True, stop=True)
                    if diag:
                        mm = nc.tensor.matmul(p_m[:, k % 2, width - P:width], cmaskb[:, 0, :],
                                              cmaskb[:, 1, :], start=False, stop=True, skip_group_check=True)
                    mm.then_inc(maxima, 1)

                def turn_maxima(g):
                    pe.wait_ge(m_all, g + 1 + FIRST)
                    pe.wait_ge(o_stored, g * 2 - 1 + FIRST)
                    rows = p_t[0:GH * TPB, :, :, :].rearrange("p a h d -> p (a h d)")[:, 0:P]
                    nc.tensor.transpose(rows, mcol[:, :], ident[:, :]).then_inc(m_turned, 1)

                def score(s, g, par, pair):
                    hq, kt, c0 = steps[s]
                    pe.wait_ge(exped, (g * (2 * NS) + (2 * s + pair - 1 if s else 0)) + FIRST)
                    for e in range(2):
                        h = 2 * pair + e
                        q0 = hq * CH + c0
                        diag = causal and kt * P >= hq * CH
                        mm = nc.tensor.matmul(p_s[:, pair, e, c0:CH], KS[:, par, h, kt * P:(kt + 1) * P],
                                              QS[:, par, h, q0:(hq + 1) * CH], start=True, stop=True)
                        if diag:
                            mm = nc.tensor.matmul(p_s[:, pair, e, c0:c0 + P], cmaskb[:, 0, :],
                                                  cmaskb[:, 2, :], start=False, stop=True,
                                                  skip_group_check=True)
                    mm.then_inc(scores, 1)

                def weigh(s, g, par):
                    hq, kt, c0 = steps[s]
                    pe.wait_ge(exped, g * (2 * NS) + 2 * s + 2 + FIRST)
                    if s == 0:
                        pe.wait_ge(v_ready, g + 3 + FIRST)
                    if kt == 0:
                        pe.wait_ge(o_kept, g * 2 + hq + FIRST)
                    for h in range(GH):
                        mm = nc.tensor.matmul(p_o[32 * h:32 * h + 32, c0:CH], V[par][:, kt, h, :],
                                              probs[:, s % 2, h, c0:CH], start=kt == 0, stop=s in ends,
                                              skip_group_check=True)
                    mm.then_inc(weighted, 1)

                def turn_out(u, maxima_before):
                    pe.wait_ge(o_kept, u + 1 + FIRST)
                    pe.wait_ge(m_split, maxima_before + FIRST)
                    pe.wait_ge(o_stored, u + FIRST)
                    for t in range(4):
                        mm = nc.tensor.transpose(p_t[:, t, :, :].rearrange("p h d -> p (h d)"),
                                                 osum[:, t * P:(t + 1) * P], ident[:, :])
                    mm.then_inc(o_turned, 1)

                pe.wait_ge(operands, 2 * 3 * GH * 16)
                for k in range(NC):
                    max_chunk(k, None, 0)
                pe.wait_ge(m_all, 1 + FIRST)
                rows0 = p_t[0:GH * TPB, :, :, :].rearrange("p a h d -> p (a h d)")[:, 0:P]
                nc.tensor.transpose(rows0, mcol[:, :], ident[:, :]).then_inc(m_turned, 1)
                with pe.Fori(0, GROUPS // 2) as i:
                    for par in range(2):
                        g = i * 2 + par
                        pe.wait_ge(m_stored, g * 48 + 48)
                        pe.wait_ge(operands, (g + 2) * (3 * GH * 16))
                        k = 0
                        for s in range(NS):
                            score(s, g, par, 0)
                            first = k
                            while k < min(NC, (s + 1) * per_step):
                                if k == first + 2:
                                    score(s, g, par, 1)
                                max_chunk(k, g + 1, 1 - par)
                                k += 1
                            if k - first <= 2:
                                score(s, g, par, 1)
                            if s == NS - 3:
                                turn_maxima(g + 1)
                            if s:
                                weigh(s - 1, g, par)
                            if s == ends[0] + 2:
                                turn_out(g * 2, g + 1)
                        weigh(NS - 1, g, par)
                        turn_out(g * 2 + 1, g + 2)

            @block.scalar
            def _(act):
                def rows_of(par, g):
                    act.wait_ge(m_split, g + 1 + FIRST)
                    for j in range(3):
                        act.dma_start(QS[KROWS + j:KROWS + j + 1, par, :, :].rearrange("p h t -> p (h t)")
                                      .rearrange("p (r c) -> p r c", c=P),
                                      mrow[:, j, :]).then_inc(m_stored, 16)

                rows_of(0, 0)
                with act.Fori(0, GROUPS // 2) as i:
                    for par in range(2):
                        g = i * 2 + par
                        for s in range(NS):
                            hq, kt, c0 = steps[s]
                            if s == NS - 1:
                                rows_of(1 - par, g + 1)
                            for pair in range(2):
                                act.wait_ge(scores, g * (2 * NS) + 2 * s + pair + 1 + FIRST)
                                if pair == 0:
                                    act.wait_ge(weighted, g * NS + max(s - 1, 0) + FIRST)
                                nc.scalar.activation(probs[:, s % 2, 2 * pair:2 * pair + 2, c0:CH],
                                                     p_s[:, pair, :, c0:CH], ACT.Exp,
                                                     scale=SM_SCALE).then_inc(exped, 1)
                act.wait_ge(m_stored, (GROUPS + 1) * 48)


def finish(nc, A, tag, XT, X0, attn, ident, ones, eps, xin, low_rank):
    with ExitStack() as ctx:
        def sb(name, shape, dt=F32):
            return ctx.enter_context(nc.sbuf_tensor(f"{tag}f_{name}", shape, dt))

        sem = semaphores(nc, ctx, f"{tag}f")

        stage = sb("stage", [P, CH])
        turned = sb("turned", [P, CH])
        low = sb("low", [RANK, CH])
        wdown = sb("wdown", [DIM, RANK])
        wup = sb("wup", [RANK, DIM])
        resid, sq, sd = sb("resid", [P, CH]), sb("sq", [P, CH]), sb("sd", [P, CH])
        p_t = ctx.enter_context(nc.psum_tensor(f"{tag}f_pt", [P, CH], F32))
        p_low = ctx.enter_context(nc.psum_tensor(f"{tag}f_plow", [P, CH], F32))
        p_y = ctx.enter_context(nc.psum_tensor(f"{tag}f_py", [P, CH], F32))
        stat = ctx.enter_context(nc.psum_tensor(f"{tag}f_stat", [P, 2, CH], F32))
        ln = {k: sem(f"ln_{k}") for k in ("resid", "mean", "sq", "var", "sd", "inv", "cent", "out", "kept")}
        weights, staged, t_done, t_kept, low_done, low_kept, y_done = (
            sem("weights", 0), sem("staged"), sem("t_done"), sem("t_kept"), sem("low_done"), sem("low_kept"),
            sem("y_done"))
        with nc.Block() as block:
            if low_rank:
                @block.sync
                def _(sp):
                    sp.dma_start(wdown[:, :], A["o_down"]).then_inc(weights, 16)
                    sp.dma_start(wup[:, :], A["o_up"]).then_inc(weights, 16)

            @block.tensor
            def _(pe):
                if low_rank:
                    pe.wait_ge(weights, 32)
                with pe.Fori(0, CHUNKS) as c:
                    pe.wait_ge(staged, c + 1 + FIRST)
                    pe.wait_ge(ln["resid"], c + FIRST)
                    for t in range(4):
                        mm = nc.tensor.transpose(p_t[:, t * P:(t + 1) * P], stage[:, t * P:(t + 1) * P],
                                                 ident[:, :])
                    mm.then_inc(t_done, 1)
                    if low_rank:
                        pe.wait_ge(t_kept, c + 1 + FIRST)
                        nc.tensor.matmul(p_low[0:RANK, :], wdown[:, :], turned[:, :], start=True,
                                         stop=True).then_inc(low_done, 1)
                        pe.wait_ge(low_kept, c + 1 + FIRST)
                        nc.tensor.matmul(p_y[:, :], wup[:, :], low[:, :], start=True,
                                         stop=True).then_inc(y_done, 1)
                    layer_norm_pe(nc, pe, stat, ones, resid, sq, ln, c)

            @block.scalar
            def _(act):
                with act.Fori(0, CHUNKS) as c:
                    if low_rank:
                        act.wait_ge(t_done, c + 1 + FIRST)
                        nc.scalar.copy(turned[:, :], p_t[:, :]).then_inc(t_kept, 1)
                        act.wait_ge(low_done, c + 1 + FIRST)
                        nc.scalar.copy(low[:, :], p_low[0:RANK, :]).then_inc(low_kept, 1)
                    layer_norm_act(nc, act, stat, sd, eps, ln, c)

            @block.vector
            def _(dve):
                with dve.Fori(0, CHUNKS) as c:
                    dve.wait_ge(t_done, c + FIRST)
                    nc.vector.tensor_copy(stage[:, :],
                                          attn[:, ds(c * 4, 4), :].rearrange("p t d -> p (t d)")).then_inc(staged, 1)
                    dve.wait_ge(y_done if low_rank else t_done, c + 1 + FIRST)
                    dve.wait_ge(ln["out"], c + FIRST)
                    x = XT[:, ds(c * CH + X0, CH)]
                    nc.vector.tensor_tensor(resid[:, :], x, (p_y if low_rank else p_t)[:, :],
                                            ALU.add).then_inc(ln["resid"], 1)
                    layer_norm_dve(nc, dve, stat, resid, sq, sd, x, ln, c,
                                   None if xin is None else xin[:, ds(c * CH, CH)])


def expert_ffn(nc, A, XT, X0, ones, eps):
    WC = 2 * FF + FF // P + 1
    B1, B2 = 2 * FF, 2 * FF + FF // P
    with ExitStack() as ctx:
        def sb(name, shape, dt=F32):
            return ctx.enter_context(nc.sbuf_tensor(f"ffn_{name}", shape, dt))

        sem = semaphores(nc, ctx, "ffn")

        base = sb("base", [P, WC])
        experts = sb("experts", [P, EXPERTS, WC])
        merged = sb("merged", [P, WC])
        gw1 = sb("gw1", [P, DIM])
        gb1 = sb("gb1", [P, 1])
        gw2 = sb("gw2", [P, EXPERTS])
        gb2 = sb("gb2", [P, EXPERTS])
        xb = sb("xb", [P, SEQ])
        hid = sb("hid", [P, CH])
        hsum = sb("hsum", [P, 2])
        hmean = sb("hmean", [P, P])
        htot = sb("htot", [P, 1])
        gate = sb("gate", [P, EXPERTS])
        u = sb("u", [P, 4, CH])
        resid, sq, sd = sb("resid", [P, CH]), sb("sq", [P, CH]), sb("sd", [P, CH])
        p_h = ctx.enter_context(nc.psum_tensor("ffn_ph", [P, CH], F32))
        p_g = ctx.enter_context(nc.psum_tensor("ffn_pg", [P, CH], F32))
        p_u = ctx.enter_context(nc.psum_tensor("ffn_pu", [P, 2, CH], F32))
        p_y = ctx.enter_context(nc.psum_tensor("ffn_py", [P, CH], F32))
        stat = ctx.enter_context(nc.psum_tensor("ffn_stat", [P, 2, CH], F32))
        ln = {k: sem(f"ln_{k}") for k in ("resid", "mean", "sq", "var", "sd", "inv", "cent", "out")}
        weights, x_in, h_done, h_sum, h_tot, h_mean, g_done, gated, merged_s = (
            sem("weights", 0), sem("x_in"), sem("h_done"), sem("h_sum"), sem("h_tot"), sem("h_mean"),
            sem("g_done"), sem("gated"), sem("merged"))
        u_done, u_kept, y_done = sem("u_done"), sem("u_kept"), sem("y_done")
        with nc.Block() as block:
            @block.sync
            def _(sp):
                for dst, name in ((gw1, "gate_w1"), (gb1, "gate_b1"), (gw2, "gate_w2"), (gb2, "gate_b2"),
                                  (base, "ffn_base")):
                    sp.dma_start(dst[:, :], A[name]).then_inc(weights, 16)
                sp.dma_start(experts[:, :, :], A["ffn_experts"]).then_inc(weights, 16)

            @block.tensor
            def _(pe):
                pe.wait_ge(weights, 96)
                with pe.Fori(0, BATCH) as b:
                    for half in range(2):
                        if half:
                            pe.wait_ge(h_sum, b * 2 + 1 + FIRST)
                        else:
                            pe.wait_ge(h_sum, b * 2 + FIRST)
                            pe.wait_ge(x_in, b + 1 + FIRST)
                        nc.tensor.matmul(p_h[:, :], gw1[:, :], xb[:, half * CH:(half + 1) * CH],
                                         start=True, stop=True).then_inc(h_done, 1)
                    pe.wait_ge(h_mean, b + 1 + FIRST)
                    nc.tensor.matmul(p_g[:, 0:EXPERTS], hmean[:, :], gw2[:, :], start=True,
                                     stop=True).then_inc(g_done, 1)
                    pe.wait_ge(merged_s, b * (EXPERTS + 0) + EXPERTS + FIRST)
                    for half in range(2):
                        for f in range(4):
                            back = half * 4 + f - 1
                            if back >= 0:
                                pe.wait_ge(u_kept, b * 8 + back + FIRST)
                            else:
                                pe.wait_ge(u_kept, b * 8 + FIRST)
                            nc.tensor.matmul(p_u[:, f % 2, :], merged[:, f * P:(f + 1) * P],
                                             xb[:, half * CH:(half + 1) * CH], start=True,
                                             stop=True).then_inc(u_done, 1)
                        pe.wait_ge(u_kept, b * 8 + (half * 4 + 4) + FIRST)
                        pe.wait_ge(ln["resid"], b * 2 + half + FIRST)
                        for f in range(4):
                            mm = nc.tensor.matmul(p_y[:, :], merged[:, FF + f * P:FF + (f + 1) * P],
                                                  u[:, f, :], start=f == 0, stop=f == 3)
                        mm.then_inc(y_done, 1)
                        layer_norm_pe(nc, pe, stat, ones, resid, sq, ln, b * 2 + half)

            @block.scalar
            def _(act):
                act.wait_ge(weights, 96)
                with act.Fori(0, BATCH) as b:
                    for half in range(2):
                        act.wait_ge(h_done, b * 2 + (half + 1) + FIRST)
                        act.wait_ge(h_tot, b + FIRST)
                        act.wait_ge(h_sum, b * 2 + half + FIRST)
                        nc.scalar.activation(hid[:, :], p_h[:, :], ACT.Relu, bias=gb1[:, 0:1],
                                             accum_out=hsum[:, half:half + 1]).then_inc(h_sum, 1)
                    for half in range(2):
                        for f in range(4):
                            act.wait_ge(u_done, b * 8 + (half * 4 + f + 1) + FIRST)
                            act.wait_ge(y_done, b * 2 + half + FIRST)
                            nc.scalar.activation(u[:, f, :], p_u[:, f % 2, :], ACT.Gelu_apprx_tanh,
                                                 bias=merged[:, B1 + f:B1 + f + 1]).then_inc(u_kept, 1)
                        layer_norm_act(nc, act, stat, sd, eps, ln, b * 2 + half)

            @block.vector
            def _(dve):
                dve.wait_ge(weights, 96)
                with dve.Fori(0, BATCH) as b:
                    dve.wait_ge(u_done, b * 8 + FIRST)
                    nc.vector.tensor_copy(xb[:, :], XT[:, ds(b * SEQ + X0, SEQ)]).then_inc(x_in, 1)
                    dve.wait_ge(h_sum, b * 2 + 2 + FIRST)
                    nc.vector.reduce_sum(htot[:, :], hsum[:, :], AX_X).then_inc(h_tot, 1)
                    dve.wait_ge(h_tot, b + 1 + FIRST)
                    nc.vector.tensor_scalar(hmean[:, :], ones[:, :], htot[:, 0:1], float(DIM) / SEQ, ALU.mult,
                                            ALU.mult).then_inc(h_mean, 1)
                    dve.wait_ge(g_done, b + 1 + FIRST)
                    nc.vector.tensor_tensor(gate[:, :], p_g[:, 0:EXPERTS], gb2[:, :], ALU.add).then_inc(gated, 1)
                    dve.wait_ge(gated, b + 1 + FIRST)
                    dve.wait_ge(ln["out"], b * 2 + FIRST)
                    for e in range(EXPERTS):
                        if e:
                            dve.wait_ge(merged_s, b * EXPERTS + e + FIRST)
                        nc.vector.scalar_tensor_tensor(
                            merged[:, :], experts[:, e, :], gate[:, e:e + 1],
                            (base if e == 0 else merged)[:, :], ALU.mult, ALU.add).then_inc(merged_s, 1)
                    for half in range(2):
                        dve.wait_ge(y_done, b * 2 + (half + 1) + FIRST)
                        dve.wait_ge(ln["out"], b * 2 + half + FIRST)
                        nc.vector.scalar_tensor_tensor(
                            resid[:, :], p_y[:, :], merged[:, B2:B2 + 1], xb[:, half * CH:(half + 1) * CH],
                            ALU.add, ALU.add).then_inc(ln["resid"], 1)
                        layer_norm_dve(nc, dve, stat, resid, sq, sd, XT[:, ds(b * SEQ + (X0 + half * CH), CH)],
                                       ln, b * 2 + half)


def windowed(nc, A, XT, ident, ones, eps):
    STEPS = TILES + 2
    KCH = [(0, P), (P, 2 * P), (2 * P, DI)]
    with ExitStack() as ctx:
        def sb(name, shape, dt=F32):
            return ctx.enter_context(nc.sbuf_tensor(f"w_{name}", shape, dt))

        sem = semaphores(nc, ctx, "w")

        def ps(name, shape):
            return ctx.enter_context(nc.psum_tensor(f"w_{name}", shape, F32))

        wqkv = sb("wqkv", [P, 3 * INNER])
        wo = sb("wo", [P, INNER // P, DIM])
        w1 = sb("w1", [P, 2 * DI])
        w2 = sb("w2", [P, 3, DIM])
        vecs = sb("vecs", [P, 10])
        scales = sb("scales", [P, 4, DH])
        rot = sb("rot", [P, 4, TPB, DH])
        tab = sb("tab", [P, 4, TPB, DH])
        wmask = sb("wmask", [P, TPB, 2 * WIN])
        notfirst = sb("notfirst", [P, TPB])

        xs = sb("xs", [P, P])
        sq = sb("sq", [P, 2, CH])
        qk = sb("qk", [P, 2, HEADS, DH])
        nrm = sb("nrm", [P, 2 * HEADS])
        t1 = sb("t1", [P, 2, HEADS, DH])
        t2 = sb("t2", [P, 2, HEADS, DH])
        qT = sb("qT", [P, HEADS // 2, P])
        kT = sb("kT", [P, HEADS // 2, WIN + P])
        vt = sb("vt", [P, INNER])
        v0 = sb("v0", [P, INNER])
        sm = sb("sm", [P, HEADS, 2 * WIN])
        mx = sb("mx", [P, HEADS])
        den = sb("den", [P, HEADS])
        pd = sb("pd", [P, HEADS, P])
        pT = sb("pT", [P, HEADS, P])
        oT = sb("oT", [P, HEADS // 2, P])
        x1 = sb("x1", [P, P + 1])
        xs2 = sb("xs2", [P, P])
        sq2 = sb("sq2", [P, P])
        sd = sb("sd", [P, P])
        gl = sb("gl", [P, 3, P])
        hid = sb("hid", [P, 3, P])

        b_proj = [ps(f"proj{j}", [P, CH]) for j in range(2)]
        b_s = [ps(f"s{j}", [P, HEADS // 2, 2 * WIN]) for j in range(2)]
        b_t = [ps(f"tb{j}", [P, 4, P]) for j in range(2)]
        b_o = ps("o", [P, 4, P])
        b_c = ps("c", [P, 4, P])

        S = {k: sem(k, 0 if k in ("consts", "weights") else FIRST) for k in (
            "consts", "weights", "cleared", "tables", "xs", "proj", "proj_kept", "k_prev", "scored0",
            "scored1", "masked", "mx", "shifted", "exped", "den", "rden", "scaled", "spread", "turn0", "turn1",
            "free0", "free1", "summed", "o_kept", "v_prev", "y", "x1", "x1p", "xs2", "mean", "cent",
            "sq2", "var", "sd", "rsd", "xn1", "xn2", "xn", "out", "x2", "nrm", "nmax", "nsd", "rn",
            "scaled_qk", "cosq", "cosk", "sinq", "sink", "rotq", "rotk", "sq_used", "loaded")}

        with nc.Block() as block:
            @block.sync
            def _(sp):
                sp.dma_start(rot[:, :, :, :], A["c_rot"]).then_inc(S["consts"], 16)
                sp.dma_start(wmask[:, :, :], A["c_wmask"]).then_inc(S["consts"], 16)
                sp.dma_start(notfirst[:, :], A["c_notfirst"]).then_inc(S["consts"], 16)
                for l in range(DEPTH):
                    if l:
                        sp.wait_ge(S["proj"], l * STEPS * 6 + FIRST)
                    sp.dma_start(wqkv[:, :], A["w_qkv"][l]).then_inc(S["weights"], 16)
                    sp.dma_start(scales[:, :, :], A["w_scales"][l]).then_inc(S["weights"], 16)
                    if l:
                        sp.wait_ge(S["x2"], l * STEPS + FIRST)
                    sp.dma_start(wo[:, :, :], A["w_o"][l]).then_inc(S["weights"], 16)
                    sp.dma_start(w1[:, :], A["w_1"][l]).then_inc(S["weights"], 16)
                    sp.dma_start(w2[:, :, :], A["w_2"][l]).then_inc(S["weights"], 16)
                    sp.dma_start(vecs[:, :], A["w_vecs"][l]).then_inc(S["weights"], 16)

            @block.gpsimd
            def _(pool):
                for tile in (qT, kT, pd, oT):
                    ms = nc.gpsimd.memset(tile[:, :, :], 0.0)
                for tile in (vt, v0, x1):
                    ms = nc.gpsimd.memset(tile[:, :], 0.0)
                ms.then_inc(S["cleared"], 1)
                with pool.Fori(0, DEPTH) as l:
                    with pool.Fori(0, STEPS) as i:
                        n = l * STEPS + i
                        pool.wait_ge(S["scaled_qk"], n + 1 + FIRST)
                        pool.wait_ge(S["rotk"], n + FIRST)
                        for half in range(2):
                            dst = slice(half * 32, half * 32 + 32)
                            src = slice(32 - half * 32, 64 - half * 32)
                            op = nc.gpsimd.tensor_tensor(
                                t2[:, 1, :, dst], qk[:, 1, :, src],
                                tab[:, 3, ds(i % TPB, 1), dst].broadcast_to([P, HEADS, 32]), ALU.mult)
                        op.then_inc(S["sink"], 1)
                        pool.wait_ge(S["cleared"], 1 + FIRST)
                        pool.wait_ge(S["scored0"], n + 1 + FIRST)
                        pool.wait_ge(S["scored1"], n + 1 + FIRST)
                        nc.gpsimd.tensor_copy(kT[:, :, 0:WIN], kT[:, :, P:P + WIN]).then_inc(S["k_prev"], 1)

            @block.tensor
            def _(pe):
                pe.wait_ge(S["cleared"], 1 + FIRST)
                with pe.Fori(0, DEPTH) as l:
                    with pe.Fori(0, STEPS) as i:
                        n = l * STEPS + i

                        def proj(c):
                            pe.wait_ge(S["proj_kept"], (n * 6 + (c - 1) if c else n * 6) + FIRST)
                            nc.tensor.matmul(b_proj[c % 2][:, :], xs[:, :], wqkv[:, c * CH:(c + 1) * CH],
                                             start=True, stop=True).then_inc(S["proj"], 1)

                        pe.wait_ge(S["weights"], l * 96 + 96)
                        pe.wait_ge(S["o_kept"], n * 2 + FIRST)
                        pe.wait_ge(S["x2"], n + FIRST)
                        for p in range(HEADS // 2):
                            if p == HEADS // 2 - 1:
                                pe.wait_ge(S["free0"], n * 5 + FIRST)
                                pe.wait_ge(S["free1"], n * 5 + FIRST)
                                pe.wait_ge(S["masked"], n * 2 + FIRST)
                            mm = nc.tensor.matmul(b_c[:, 0, :], wo[:, p, :], oT[:, p, :], start=p == 0,
                                                  stop=p == HEADS // 2 - 1)
                        mm.then_inc(S["y"], 1)
                        for p in range(HEADS // 2):
                            for e in range(2):
                                r = slice(64 * e, 64 * e + 64)
                                for w in range(4):
                                    mm = nc.tensor.matmul(
                                        b_s[e][32 * w:32 * w + 32, p, :], qT[r, p, 32 * w:32 * w + 32],
                                        kT[r, p, 32 * w:32 * w + 64], start=True, stop=True)
                                if p == HEADS // 2 - 1:
                                    mm.then_inc(S[f"scored{e}"], 1)
                        pe.wait_ge(S["xs"], n + 1 + FIRST)
                        proj(0)
                        proj(1)
                        pe.wait_ge(S["xs2"], n + 1 + FIRST)
                        nc.tensor.matmul(b_c[:, 1, :], ones[:, :], xs2[:, :], start=True,
                                         stop=True).then_inc(S["mean"], 1)
                        proj(2)
                        pe.wait_ge(S["sq2"], n + 1 + FIRST)
                        nc.tensor.matmul(b_c[:, 2, :], ones[:, :], sq2[:, :], start=True,
                                         stop=True).then_inc(S["var"], 1)
                        proj(3)
                        pe.wait_ge(S["spread"], n + 1 + FIRST)
                        for grp in range(4):
                            j = grp % 2
                            pe.wait_ge(S[f"free{j}"], n * 5 + grp // 2 + FIRST)
                            for k in range(4):
                                mm = nc.tensor.transpose(b_t[j][:, k, :], pd[:, 4 * grp + k, :], ident[:, :])
                            mm.then_inc(S[f"turn{j}"], 1)
                        pe.wait_ge(S["xn"], n + 1 + FIRST)
                        for j, off in ((0, DI), (1, 0)):
                            pe.wait_ge(S[f"free{j}"], n * 5 + 2 + FIRST)
                            for k, (lo, hi) in enumerate(KCH):
                                mm = nc.tensor.matmul(b_t[j][0:hi - lo, k, :], w1[:, off + lo:off + hi],
                                                      xs2[:, :], start=True, stop=True)
                            mm.then_inc(S[f"turn{j}"], 1)
                        for half in range(2):
                            pe.wait_ge(S["o_kept"], n * 2 + half + FIRST)
                            for k in range(4):
                                p = 4 * half + k
                                for cols, val in ((slice(WIN, P), vt), (slice(0, WIN), v0)):
                                    for e in range(2):
                                        f = (2 * p + e) * DH
                                        mm = nc.tensor.matmul(b_o[64 * e:64 * e + 64, k, cols],
                                                              val[:, f:f + DH],
                                                              pT[:, e * 8 + p, cols],
                                                              start=True, stop=True)
                            mm.then_inc(S["summed"], 1)
                        proj(4)
                        proj(5)
                        pe.wait_ge(S["free1"], n * 5 + 3 + FIRST)
                        for k, (lo, hi) in enumerate(KCH):
                            mm = nc.tensor.matmul(b_c[:, 3, :], w2[0:hi - lo, k, :], hid[0:hi - lo, k, :],
                                                  start=k == 0, stop=k == 2)
                        mm.then_inc(S["out"], 1)
                        for grp in range(4):
                            j = grp % 2
                            pe.wait_ge(S["rotq" if grp < 2 else "rotk"], n + 1 + FIRST)
                            pe.wait_ge(S[f"free{j}"], n * 5 + (3 + grp // 2) + FIRST)
                            for k in range(4):
                                src = t1[:, grp // 2, :, :].rearrange("p h d -> p (h d)")
                                c0 = (4 * (grp % 2) + k) * P
                                mm = nc.tensor.transpose(b_t[j][:, k, :], src[:, c0:c0 + P], ident[:, :])
                            mm.then_inc(S[f"turn{j}"], 1)

            @block.scalar
            def _(act):
                act.wait_ge(S["cleared"], 1 + FIRST)
                with act.Fori(0, DEPTH) as l:
                    act.wait_ge(S["weights"], l * 96 + 96)
                    with act.Fori(0, STEPS) as i:
                        n = l * STEPS + i

                        def keep(c):
                            act.wait_ge(S["proj"], n * 6 + (c + 1) + FIRST)
                            if c == 0:
                                act.wait_ge(S["rotk"], n + FIRST)
                                act.wait_ge(S["sinq"], n + FIRST)
                                act.wait_ge(S["sink"], n + FIRST)
                            act.wait_ge(S["sq_used"], (n * 4 + (c - 1) if c else n * 4) + FIRST)
                            nc.scalar.square(sq[:, c % 2, :], b_proj[c % 2][:, :]).then_inc(S["loaded"], 1)
                            nc.scalar.copy(qk[:, c // 2, 8 * (c % 2):8 * (c % 2) + 8, :].rearrange("p h d -> p (h d)"),
                                           b_proj[c % 2][:, :]).then_inc(S["proj_kept"], 1)

                        keep(0)
                        keep(1)
                        act.wait_ge(S["shifted"], n + 1 + FIRST)
                        nc.scalar.activation(sm[:, :, :], sm[:, :, :], ACT.Exp).then_inc(S["exped"], 1)
                        keep(2)
                        keep(3)
                        act.wait_ge(S["scaled"], n + 1 + FIRST)
                        for w in range(4):
                            r = slice(32 * w, 32 * w + 32)
                            if w == 0:
                                nc.scalar.copy(pd[r, :, 96:128], sm[r, :, 0:32])
                                nc.scalar.copy(pd[r, :, 0:32], sm[r, :, 32:64])
                            else:
                                op = nc.scalar.copy(pd[r, :, 32 * w - 32:32 * w + 32], sm[r, :, :])
                        op.then_inc(S["spread"], 1)
                        act.wait_ge(S["var"], n + 1 + FIRST)
                        act.wait_ge(S["rsd"], n + FIRST)
                        nc.scalar.activation(sd[:, :], b_c[:, 2, :], ACT.Sqrt, bias=eps[:, 0:1]).then_inc(S["sd"], 1)
                        act.wait_ge(S["nmax"], n + 1 + FIRST)
                        nc.scalar.activation(nrm[:, :], nrm[:, :], ACT.Sqrt).then_inc(S["nsd"], 1)
                        for k in range(2):
                            act.wait_ge(S["turn0"], n * 5 + (k + 1) + FIRST)
                            if k == 0:
                                act.wait_ge(S["summed"], n * 2 + FIRST)
                            nc.scalar.copy(pT[:, 8 * k:8 * k + 4, :], b_t[0][:, :, :]).then_inc(S["free0"], 1)
                        act.wait_ge(S["turn0"], n * 5 + 3 + FIRST)
                        act.wait_ge(S["free1"], n * 5 + FIRST)
                        for k, (lo, hi) in enumerate(KCH):
                            op = nc.scalar.activation(gl[0:hi - lo, k, :], b_t[0][0:hi - lo, k, :], ACT.Gelu,
                                                      bias=vecs[0:hi - lo, 7 + k:8 + k])
                        op.then_inc(S["free0"], 1)
                        act.wait_ge(S["y"], n + 1 + FIRST)
                        for half in range(2):
                            act.wait_ge(S["summed"], n * 2 + (half + 1) + FIRST)
                            nc.scalar.copy(oT[:, 4 * half:4 * half + 4, :], b_o[:, :, :]).then_inc(S["o_kept"], 1)
                        act.wait_ge(S["v_prev"], n + 1 + FIRST)
                        for c in (4, 5):
                            cols = slice((c - 4) * CH, (c - 3) * CH)
                            act.wait_ge(S["proj"], n * 6 + (c + 1) + FIRST)
                            nc.scalar.copy(v0[0:WIN, cols], b_proj[c % 2][0:WIN, :])
                            nc.scalar.copy(vt[:, cols], b_proj[c % 2][:, :]).then_inc(S["proj_kept"], 1)
                        act.wait_ge(S["k_prev"], n + 1 + FIRST)
                        for k in range(2):
                            act.wait_ge(S["turn0"], n * 5 + (4 + k) + FIRST)
                            dst = qT[:, 0:4, :] if k == 0 else kT[:, 0:4, WIN:WIN + P]
                            op = nc.scalar.copy(dst, b_t[0][:, :, :])
                            op.then_inc(S["free0"], 1)

            @block.vector
            def _(dve):
                dve.wait_ge(S["consts"], 48)
                dve.wait_ge(S["cleared"], 1 + FIRST)
                with dve.Fori(0, DEPTH) as l:
                    dve.wait_ge(S["weights"], l * 96 + 96)
                    dve.wait_ge(S["sink"], l * STEPS + FIRST)
                    for j in range(4):
                        op = nc.vector.tensor_tensor(
                            tab[:, j, :, :], rot[:, j, :, :],
                            scales[:, j:j + 1, :].broadcast_to([P, TPB, DH]), ALU.mult)
                    op.then_inc(S["tables"], 1)
                    with dve.Fori(0, STEPS) as i:
                        n = l * STEPS + i
                        dve.wait_ge(S["tables"], l + 1 + FIRST)
                        dve.wait_ge(S["proj"], n * 6 + FIRST)
                        nc.vector.tensor_copy(xs[0:64, :], XT[0:64, ds(i * P + PADL * P, P)])
                        nc.vector.tensor_copy(xs[64:128, 1:P], XT[64:128, ds(i * P + PADL * P, P - 1)])
                        nc.vector.tensor_tensor(xs[64:128, 0:1], XT[64:128, ds(i * P + (PADL * P - 1), 1)],
                                                notfirst[64:128, ds(i % TPB, 1)], ALU.mult).then_inc(S["xs"], 1)
                        nc.vector.tensor_tensor(x1[64:128, 0:1], x1[64:128, P:P + 1],
                                                notfirst[64:128, ds((i + 6) % TPB, 1)],
                                                ALU.mult).then_inc(S["x1p"], 1)
                        dve.wait_ge(S["y"], n + 1 + FIRST)
                        dve.wait_ge(S["x1p"], n + 1 + FIRST)
                        nc.vector.tensor_tensor(x1[:, 1:P + 1], XT[:, ds(i * P, P)], b_c[:, 0, :],
                                                ALU.add).then_inc(S["x1"], 1)
                        dve.wait_ge(S["x1"], n + 1 + FIRST)
                        nc.vector.tensor_copy(xs2[0:64, :], x1[0:64, 1:P + 1])
                        nc.vector.tensor_copy(xs2[64:128, :], x1[64:128, 0:P]).then_inc(S["xs2"], 1)
                        for e in range(2):
                            dve.wait_ge(S[f"scored{e}"], n + 1 + FIRST)
                            if e == 0:
                                dve.wait_ge(S["spread"], n + FIRST)
                            nc.vector.tensor_tensor(
                                sm[:, 8 * e:8 * e + 8, :], b_s[e][:, :, :],
                                wmask[:, ds((i + 7) % TPB, 1), :].broadcast_to([P, 8, 2 * WIN]),
                                ALU.add).then_inc(S["masked"], 1)
                        dve.wait_ge(S["masked"], n * 2 + 2 + FIRST)
                        nc.vector.reduce_max(mx[:, :], sm[:, :, :], AX_X).then_inc(S["mx"], 1)
                        dve.wait_ge(S["mx"], n + 1 + FIRST)
                        nc.vector.tensor_tensor(
                            sm[:, :, :], sm[:, :, :], mx[:, :].unsqueeze(2).broadcast_to([P, HEADS, 2 * WIN]),
                            ALU.subtract).then_inc(S["shifted"], 1)
                        dve.wait_ge(S["mean"], n + 1 + FIRST)
                        nc.vector.tensor_tensor(xs2[:, :], xs2[:, :], b_c[:, 1, :], ALU.subtract).then_inc(S["cent"], 1)
                        dve.wait_ge(S["cent"], n + 1 + FIRST)
                        nc.vector.tensor_tensor(sq2[:, :], xs2[:, :], xs2[:, :], ALU.mult).then_inc(S["sq2"], 1)

                        def norms(c):
                            dve.wait_ge(S["loaded"], n * 4 + (c + 1) + FIRST)
                            if c == 0:
                                dve.wait_ge(S["rn"], n + FIRST)
                            nc.vector.reduce_sum(nrm[:, 8 * c:8 * c + 8],
                                                 sq[:, c % 2, :].rearrange("p (h d) -> p h d", h=8),
                                                 AX_X).then_inc(S["sq_used"], 1)

                        norms(0)
                        norms(1)
                        dve.wait_ge(S["exped"], n + 1 + FIRST)
                        nc.vector.reduce_sum(den[:, :], sm[:, :, :], AX_X).then_inc(S["den"], 1)
                        dve.wait_ge(S["den"], n + 1 + FIRST)
                        nc.vector.reciprocal(den[:, :], den[:, :]).then_inc(S["rden"], 1)
                        dve.wait_ge(S["rden"], n + 1 + FIRST)
                        nc.vector.tensor_tensor(
                            sm[:, :, :], sm[:, :, :], den[:, :].unsqueeze(2).broadcast_to([P, HEADS, 2 * WIN]),
                            ALU.mult).then_inc(S["scaled"], 1)
                        norms(2)
                        norms(3)
                        dve.wait_ge(S["sq_used"], n * 4 + 4 + FIRST)
                        nc.vector.tensor_scalar(nrm[:, :], nrm[:, :], 1e-24, None, ALU.max).then_inc(S["nmax"], 1)
                        dve.wait_ge(S["sd"], n + 1 + FIRST)
                        nc.vector.reciprocal(sd[:, :], sd[:, :]).then_inc(S["rsd"], 1)
                        dve.wait_ge(S["rsd"], n + 1 + FIRST)
                        nc.vector.tensor_tensor(xs2[:, :], xs2[:, :], sd[:, :], ALU.mult).then_inc(S["xn1"], 1)
                        dve.wait_ge(S["xn1"], n + 1 + FIRST)
                        nc.vector.tensor_scalar(xs2[:, :], xs2[:, :], vecs[:, 0:1], vecs[:, 1:2], ALU.mult,
                                                ALU.add).then_inc(S["xn"], 1)
                        dve.wait_ge(S["nsd"], n + 1 + FIRST)
                        nc.vector.reciprocal(nrm[:, :], nrm[:, :]).then_inc(S["rn"], 1)
                        dve.wait_ge(S["rn"], n + 1 + FIRST)
                        dve.wait_ge(S["proj_kept"], n * 6 + 4 + FIRST)
                        flat = qk[:, :, :, :].rearrange("p a h d -> p (a h) d")
                        nc.vector.tensor_tensor(
                            flat, flat, nrm[:, :].unsqueeze(2).broadcast_to([P, 2 * HEADS, DH]),
                            ALU.mult).then_inc(S["scaled_qk"], 1)
                        for k in range(2):
                            dve.wait_ge(S["turn1"], n * 5 + (k + 1) + FIRST)
                            if k == 0:
                                dve.wait_ge(S["summed"], n * 2 + FIRST)
                            nc.vector.tensor_copy(pT[:, 8 * k + 4:8 * k + 8, :], b_t[1][:, :, :]).then_inc(S["free1"], 1)
                        dve.wait_ge(S["turn1"], n * 5 + 3 + FIRST)
                        dve.wait_ge(S["free0"], n * 5 + 3 + FIRST)
                        for k, (lo, hi) in enumerate(KCH):
                            op = nc.vector.scalar_tensor_tensor(
                                hid[0:hi - lo, k, :], b_t[1][0:hi - lo, k, :], vecs[0:hi - lo, 4 + k:5 + k],
                                gl[0:hi - lo, k, :], ALU.add, ALU.mult)
                        op.then_inc(S["free1"], 1)
                        dve.wait_ge(S["scaled_qk"], n + 1 + FIRST)
                        dve.wait_ge(S["turn0"], n * 5 + FIRST)
                        dve.wait_ge(S["turn1"], n * 5 + FIRST)
                        for half in range(2):
                            dst = slice(half * 32, half * 32 + 32)
                            src = slice(32 - half * 32, 64 - half * 32)
                            op = nc.vector.tensor_tensor(
                                t2[:, 0, :, dst], qk[:, 0, :, src],
                                tab[:, 1, ds(i % TPB, 1), dst].broadcast_to([P, HEADS, 32]), ALU.mult)
                        op.then_inc(S["sinq"], 1)
                        for a, (cos, sin, done) in enumerate((("cosq", "sinq", "rotq"), ("cosk", "sink", "rotk"))):
                            nc.vector.tensor_tensor(
                                t1[:, a, :, :], qk[:, a, :, :],
                                tab[:, 2 * a, ds(i % TPB, 1), :].broadcast_to([P, HEADS, DH]),
                                ALU.mult).then_inc(S[cos], 1)
                            dve.wait_ge(S[cos], n + 1 + FIRST)
                            dve.wait_ge(S[sin], n + 1 + FIRST)
                            nc.vector.tensor_tensor(t1[:, a, :, :], t1[:, a, :, :], t2[:, a, :, :],
                                                    ALU.add).then_inc(S[done], 1)
                        dve.wait_ge(S["summed"], n * 2 + 2 + FIRST)
                        nc.vector.tensor_copy(v0[96:128, :], vt[96:128, :]).then_inc(S["v_prev"], 1)
                        dve.wait_ge(S["out"], n + 1 + FIRST)
                        nc.vector.scalar_tensor_tensor(
                            XT[:, ds(i * P, P)], b_c[:, 3, :], vecs[:, 2:3], x1[:, 1:P + 1], ALU.add,
                            ALU.add).then_inc(S["x2"], 1)
                        dve.wait_ge(S["k_prev"], n + 1 + FIRST)
                        dve.wait_ge(S["x2"], n + 1 + FIRST)
                        for k in range(2):
                            dve.wait_ge(S["turn1"], n * 5 + (4 + k) + FIRST)
                            dst = qT[:, 4:8, :] if k == 0 else kT[:, 4:8, WIN:WIN + P]
                            nc.vector.tensor_copy(dst, b_t[1][:, :, :]).then_inc(S["free1"], 1)


def last_norm(nc, XT, X0, xin, ones, eps, out_dram):
    with ExitStack() as ctx:
        def sb(name, shape, dt=F32):
            return ctx.enter_context(nc.sbuf_tensor(f"last_{name}", shape, dt))

        sem = semaphores(nc, ctx, "last")
        resid, sq, sd = sb("resid", [P, CH]), sb("sq", [P, CH]), sb("sd", [P, CH])
        stat = ctx.enter_context(nc.psum_tensor("last_stat", [P, 2, CH], F32))
        ln = {k: sem(f"ln_{k}") for k in ("resid", "mean", "sq", "var", "sd", "inv", "cent", "out")}
        stored = sem("stored", 0)
        with nc.Block() as block:
            @block.sync
            def _(sp):
                for c in range(CHUNKS):
                    sp.wait_ge(ln["out"], c + 1 + FIRST)
                    sp.dma_start(out_dram[:, c * CH:(c + 1) * CH],
                                 xin[:, c * CH:(c + 1) * CH]).then_inc(stored, 16)
                sp.wait_ge(stored, CHUNKS * 16)

            @block.tensor
            def _(pe):
                with pe.Fori(0, CHUNKS) as c:
                    layer_norm_pe(nc, pe, stat, ones, resid, sq, ln, c)

            @block.scalar
            def _(act):
                with act.Fori(0, CHUNKS) as c:
                    layer_norm_act(nc, act, stat, sd, eps, ln, c)

            @block.vector
            def _(dve):
                with dve.Fori(0, CHUNKS) as c:
                    dve.wait_ge(ln["out"], c + FIRST)
                    nc.vector.tensor_tensor(resid[:, :], XT[:, ds(c * CH + X0, CH)],
                                            xin[:, ds(c * CH, CH)], ALU.add).then_inc(ln["resid"], 1)
                    layer_norm_dve(nc, dve, stat, resid, sq, sd, xin[:, ds(c * CH, CH)], ln, c)


def shape_constants():
    f32 = np.float32
    ident = np.eye(P, dtype=f32)
    k, q = np.arange(P)[:, None], np.arange(P)[None, :]
    causal = np.stack([ident, np.where(q > k, f32(NEG), f32(0)), np.where(k > q, f32(NEG), f32(0))], 1).astype(f32)
    r = np.arange(P) % WIN
    c = np.arange(WIN)
    before = np.where(c[None, :] < r[:, None], f32(NEG), f32(0))
    own = np.where(c[None, :] > r[:, None], f32(NEG), f32(0))
    wmask = np.repeat(np.concatenate([before, own], 1)[:, None, :], TPB, 1).astype(f32)
    wmask[0:WIN, 0, 0:WIN] = NEG
    notfirst = np.ones((P, TPB), f32)
    notfirst[:, 0] = 0
    half = np.arange(0, DH, 2, dtype=f32)
    inv_freq = (f32(1.0) / f32(10000.0) ** (half / f32(DH))).astype(f32)
    t = np.arange(SEQ, dtype=f32)
    freqs = (t[:, None] * inv_freq[None, :]).astype(f32)
    freqs = np.concatenate([freqs, freqs], -1)
    base = ((half + f32(0.4 * DH)) / f32(1.4 * DH)).astype(f32)
    power = ((t - SEQ // 2) / f32(WIN // 2)).astype(f32)
    scale = (base[None, :] ** power[:, None]).astype(f32)
    scale = np.concatenate([scale, scale], -1)
    cos, sin = np.cos(freqs).astype(f32), np.sin(freqs).astype(f32)
    sin[:, :DH // 2] *= -1
    inv = f32(1.0) / scale
    rot = np.stack([cos * scale * 8, sin * scale * 8, cos * inv, sin * inv], 0).astype(f32)
    rot = rot.reshape(4, TPB, P, DH).transpose(2, 0, 1, 3)
    return {"c_ident": ident, "c_causal": causal, "c_wmask": wmask, "c_notfirst": notfirst, "c_rot": rot}


def layout(i):
    T = lambda a: a.T
    swap = lambda a: np.concatenate([a[:, DH // 2:], a[:, :DH // 2]], 1)
    rep = lambda a: np.broadcast_to(a[..., None, :], a.shape[:-1] + (P,) + a.shape[-1:])

    def ffn(w1, w2, b1, b2):
        return np.concatenate([w1.T, w2.T.reshape(4, P, DIM).transpose(1, 0, 2).reshape(P, FF),
                               b1.reshape(4, P).T, b2[:, None]], 1)

    def pieces(v):
        out = np.zeros((DEPTH, P, 3), v.dtype)
        for k in range(3):
            piece = v[:, k * P:(k + 1) * P]
            out[:, :piece.shape[1], k] = piece
        return out

    w2 = np.zeros((DEPTH, 3 * P, DIM), np.float32)
    w2[:, :DI] = i["L1_ffn_W2"]
    b1 = i["L1_ffn_b1"]
    qs, ks = i["L1_ffn_q_scale"], i["L1_ffn_k_scale"]
    experts = np.stack([ffn(i["L0_ffn_TW1"][e], i["L0_ffn_TW2"][e], i["L0_ffn_Tb1"][e], i["L0_ffn_Tb2"][e])
                        for e in range(EXPERTS)], 1)
    return {
        "x": T(i["L0_attn_x"].reshape(TOKENS, DIM)),
        "qkv_down": T(i["L0_attn_W_qkv_v"]), "qkv_up": T(i["L0_attn_W_qkv_u"]),
        "o_down": T(i["L0_attn_W_o_v"]), "o_up": T(i["L0_attn_W_o_u"]),
        "gate_w1": T(i["L0_ffn_gate_w1"]), "gate_b1": i["L0_ffn_gate_b1"][:, None],
        "gate_w2": T(i["L0_ffn_gate_w2"]), "gate_b2": rep(i["L0_ffn_gate_b2"]),
        "ffn_base": ffn(i["L0_ffn_W1"], i["L0_ffn_W2"], i["L0_ffn_b1"], i["L0_ffn_b2"]),
        "ffn_experts": experts,
        "wq": i["L1_attn_Wq"], "wk": i["L1_attn_Wk"], "wv": i["L1_attn_Wv"],
        "w_qkv": i["L1_ffn_Wqkv"],
        "w_scales": rep(np.stack([qs, swap(qs), ks, swap(ks)], 1).reshape(DEPTH, 4 * DH)).reshape(DEPTH, P, 4, DH),
        "w_o": i["L1_ffn_Wo"].reshape(DEPTH, INNER // P, P, DIM).transpose(0, 2, 1, 3),
        "w_1": i["L1_ffn_W1"],
        "w_2": w2.reshape(DEPTH, 3, P, DIM).transpose(0, 2, 1, 3),
        "w_vecs": np.concatenate([i["L1_ffn_ln_g"][:, :, None], i["L1_ffn_ln_b"][:, :, None],
                                  i["L1_ffn_b2"][:, :, None], np.zeros((DEPTH, P, 1), np.float32),
                                  pieces(b1[:, :DI]), pieces(b1[:, DI:])], 2),
    }


def kernel(**inputs):
    import concourse.bacc as _bacc
    from concourse.bass_utils import run_bass_kernel_spmd as _run

    nc = _bacc.Bacc("TRN2", target_bir_lowering=False, num_devices=1)
    arrays = {f"in_{k}": np.ascontiguousarray(v)
              for k, v in {**layout({k: np.asarray(v) for k, v in inputs.items()}), **shape_constants()}.items()}
    A = {k[3:]: nc.dram_tensor(k, v.shape, mybir.dt.from_np(v.dtype), kind="ExternalInput").ap()
         for k, v in arrays.items()}
    out = nc.dram_tensor("out_dram", (DIM, TOKENS), F32, kind="ExternalOutput").ap()
    build(nc, A, out)
    r = _run(nc, [arrays], core_ids=[0])
    return np.ascontiguousarray(r.results[0]["out_dram"].T).reshape(BATCH, SEQ, DIM)
```

```python
from contextlib import ExitStack

import concourse.bass as bass
import numpy as np
from concourse import mybir

F32 = mybir.dt.float32
BF16 = mybir.dt.bfloat16
ALU = mybir.AluOpType
ACT = mybir.ActivationFunctionType
AX_X = mybir.AxisListType.X

P = 128
BATCH, SEQ, DIM = 4, 1024, 128
TOKENS = BATCH * SEQ
TILES = TOKENS // P
TPB = SEQ // P
CH = 512
CHUNKS = TOKENS // CH
HEADS = 16
HD = DIM // HEADS
RANK = 32
FF, EXPERTS = 512, 8
DEPTH, DH, WIN = 6, 64, 32
INNER = HEADS * DH
DI = int(DIM * 4 * 2 / 3)
EPS = 1e-5
PADL = 3
SLOTS = PADL + TILES + PADL
NEG = -3.0e38
PARTS = 6
Q_PART = (0, 0, 1, 1, 0, 2)
K_PART = (0, 1, 0, 1, 2, 0)
KROWS = PARTS * HD
GH = 4
GROUPS = BATCH * HEADS // GH
SM_SCALE = 1.0 / float(np.sqrt(np.float32(HD)))


FIRST = 1


def ds(start, n):
    return bass.ds(start, n)


def semaphores(nc, ctx, tag):
    taken = []

    def clear():
        nc.clear_and_free_semaphores(taken)
        nc.all_engine_barrier()

    def sem(name, start=FIRST):
        taken.append(nc.alloc_semaphore(f"{tag}_{name}"))
        if start:
            nc.sync.sem_inc(taken[-1], start)
        return taken[-1]

    ctx.callback(clear)
    return sem


def layer_norm_pe(nc, pe, stat, ones, resid, sq, ln, n):
    pe.wait_ge(ln["resid"], n + 1 + FIRST)
    nc.tensor.matmul(stat[:, 0, :], ones[:, :], resid[:, :], start=True, stop=True).then_inc(ln["mean"], 1)
    pe.wait_ge(ln["sq"], n + 1 + FIRST)
    nc.tensor.matmul(stat[:, 1, :], ones[:, :], sq[:, :], start=True, stop=True).then_inc(ln["var"], 1)


def layer_norm_act(nc, act, stat, sd, eps, ln, n):
    act.wait_ge(ln["var"], n + 1 + FIRST)
    act.wait_ge(ln["inv"], n + FIRST)
    nc.scalar.activation(sd[:, :], stat[:, 1, :], ACT.Sqrt, bias=eps[:, 0:1]).then_inc(ln["sd"], 1)


def layer_norm_dve(nc, dve, stat, resid, sq, sd, out, ln, n, extra=None):
    dve.wait_ge(ln["mean"], n + 1 + FIRST)
    nc.vector.tensor_tensor(resid[:, :], resid[:, :], stat[:, 0, :], ALU.subtract).then_inc(ln["cent"], 1)
    dve.wait_ge(ln["cent"], n + 1 + FIRST)
    nc.vector.tensor_tensor(sq[:, :], resid[:, :], resid[:, :], ALU.mult).then_inc(ln["sq"], 1)
    dve.wait_ge(ln["sd"], n + 1 + FIRST)
    nc.vector.reciprocal(sd[:, :], sd[:, :]).then_inc(ln["inv"], 1)
    dve.wait_ge(ln["inv"], n + 1 + FIRST)
    nc.vector.tensor_tensor(out, resid[:, :], sd[:, :], ALU.mult).then_inc(ln["out"], 1)
    if extra is not None:
        dve.wait_ge(ln["out"], n + 1 + FIRST)
        nc.vector.tensor_copy(extra, out).then_inc(ln["kept"], 1)


def build(nc, A, out_dram):
    with ExitStack() as whole:
        def keep(name, shape, dt=F32):
            return whole.enter_context(nc.sbuf_tensor(name, shape, dt))

        XT = keep("XT", [P, SLOTS * P])
        X0 = PADL * P
        xin = keep("xin", [P, TOKENS])
        ident = keep("ident", [P, P])
        ones = keep("ones", [P, P])
        eps = keep("eps", [P, 1])
        q_parts = nc.dram_tensor("q_parts", [BATCH * P, PARTS, SEQ], BF16, kind="Internal").ap()
        k_parts = nc.dram_tensor("k_parts", [BATCH * P, PARTS, SEQ], BF16, kind="Internal").ap()

        with ExitStack() as ctx:
            loaded = semaphores(nc, ctx, "s0")("loaded", 0)
            with nc.Block() as block:
                @block.sync
                def _(sp):
                    sp.dma_start(XT[:, X0:X0 + TOKENS], A["x"]).then_inc(loaded, 16)
                    sp.dma_start(ident[:, :], A["c_ident"]).then_inc(loaded, 16)
                    sp.wait_ge(loaded, 32)

                @block.vector
                def _(dve):
                    nc.vector.memset(ones[:, :], 1.0 / DIM)
                    nc.vector.memset(eps[:, :], EPS)
                    nc.vector.memset(XT[:, 0:X0], 0.0)
                    nc.vector.memset(XT[:, X0 + TOKENS:SLOTS * P], 0.0)

        with ExitStack() as ctx:
            vals = ctx.enter_context(nc.sbuf_tensor("a1_vals", [P, TILES, HEADS, HD + 1], F32))
            attn = ctx.enter_context(nc.sbuf_tensor("a1_attn", [P, TILES, DIM], F32))
            project(nc, A, "a1", XT, X0, vals, q_parts, k_parts, low_rank=True)
            attention(nc, A, "a1", vals, attn, q_parts, k_parts, ident, causal=False)
            finish(nc, A, "a1", XT, X0, attn, ident, ones, eps, None, low_rank=True)
        expert_ffn(nc, A, XT, X0, ones, eps)
        with ExitStack() as ctx:
            vals = ctx.enter_context(nc.sbuf_tensor("a2_vals", [P, TILES, HEADS, HD + 1], F32))
            attn = ctx.enter_context(nc.sbuf_tensor("a2_attn", [P, TILES, DIM], F32))
            project(nc, A, "a2", XT, X0, vals, q_parts, k_parts, low_rank=False)
            attention(nc, A, "a2", vals, attn, q_parts, k_parts, ident, causal=True)
            finish(nc, A, "a2", XT, X0, attn, ident, ones, eps, xin, low_rank=False)
        windowed(nc, A, XT, ident, ones, eps)
        last_norm(nc, XT, X0, xin, ones, eps, out_dram)


def project(nc, A, tag, XT, X0, vals, q_parts, k_parts, low_rank):
    with ExitStack() as ctx:
        def sb(name, shape, dt=F32):
            return ctx.enter_context(nc.sbuf_tensor(f"{tag}p_{name}", shape, dt))

        sem = semaphores(nc, ctx, f"{tag}p")

        KD = RANK if low_rank else DIM
        wdown = sb("wdown", [DIM, RANK])
        w = sb("w", [KD, 3 * DIM])
        src = sb("src", [KD, CH])
        part = sb("part", [P, 2, 3, CH], BF16)
        rest = sb("rest", [P, 2, 2, CH])
        p_src = ctx.enter_context(nc.psum_tensor(f"{tag}p_psrc", [P, CH], F32))
        p_qk = ctx.enter_context(nc.psum_tensor(f"{tag}p_pqk", [P, 2, CH], F32))
        p_v = ctx.enter_context(nc.psum_tensor(f"{tag}p_pv", [P, 4, DIM], F32))
        weights, down, src_ready = sem("weights", 0), sem("down"), sem("src_ready")
        projected, first, rest1 = sem("projected"), sem("first"), sem("rest1")
        second, third, v_ready, v_kept = sem("second"), sem("third"), sem("v_ready"), sem("v_kept")
        stored = [sem("q_stored", 0), sem("k_stored", 0)]
        with nc.Block() as block:
            @block.sync
            def _(sp):
                if low_rank:
                    sp.dma_start(wdown[:, :], A["qkv_down"]).then_inc(weights, 16)
                    sp.dma_start(w[:, :], A["qkv_up"]).then_inc(weights, 16)
                else:
                    sp.dma_start(w[:, 0:DIM], A["wq"]).then_inc(weights, 16)
                    sp.dma_start(w[:, DIM:2 * DIM], A["wk"]).then_inc(weights, 16)
                    sp.dma_start(w[:, 2 * DIM:3 * DIM], A["wv"]).then_inc(weights, 16)
                for c in range(CHUNKS):
                    b, col = c // 2, c % 2 * CH
                    for s, (order, dst) in enumerate(((Q_PART, q_parts), (K_PART, k_parts))):
                        sp.wait_ge(third, 2 * c + s + 1 + FIRST)
                        for g, j in enumerate(order):
                            sp.dma_start(dst[b * P:(b + 1) * P, g, col:col + CH],
                                         part[:, s, j, :]).then_inc(stored[s], 16)
                for s in range(2):
                    sp.wait_ge(stored[s], CHUNKS * PARTS * 16)

            @block.tensor
            def _(pe):
                pe.wait_ge(weights, 32 if low_rank else 48)
                with pe.Fori(0, CHUNKS) as c:
                    if low_rank:
                        pe.wait_ge(src_ready, c + FIRST)
                        nc.tensor.matmul(p_src[0:RANK, :], wdown[:, :], XT[:, ds(c * CH + X0, CH)],
                                         start=True, stop=True).then_inc(down, 1)
                    pe.wait_ge(src_ready, c + 1 + FIRST)
                    pe.wait_ge(third, 2 * c + FIRST)
                    for s in range(2):
                        nc.tensor.matmul(p_qk[:, s, :], w[:, s * DIM:(s + 1) * DIM], src[:, :],
                                         start=True, stop=True).then_inc(projected, 1)
                    pe.wait_ge(v_kept, c + FIRST)
                    for t in range(4):
                        mm = nc.tensor.matmul(p_v[:, t, :], src[:, t * P:(t + 1) * P],
                                              w[:, 2 * DIM:3 * DIM], start=True, stop=True)
                    mm.then_inc(v_ready, 1)

            @block.scalar
            def _(act):
                with act.Fori(0, CHUNKS) as c:
                    if low_rank:
                        act.wait_ge(down, c + 1 + FIRST)
                        act.wait_ge(v_ready, c + FIRST)
                        nc.scalar.copy(src[:, :], p_src[0:RANK, :]).then_inc(src_ready, 1)
                    else:
                        act.wait_ge(v_ready, c + FIRST)
                        nc.scalar.copy(src[:, :], XT[:, ds(c * CH + X0, CH)]).then_inc(src_ready, 1)
                    act.wait_ge(v_ready, c + 1 + FIRST)
                    nc.scalar.copy(vals[:, ds(c * 4, 4), :, 0:HD],
                                   p_v[:, :, :].rearrange("p t (h d) -> p t h d", h=HEADS)).then_inc(v_kept, 1)

            @block.vector
            def _(dve):
                ones_col = vals[:, :, :, HD:HD + 1].rearrange("p t h o -> p (t h) o")
                nc.vector.memset(ones_col, 1.0)
                for c in range(CHUNKS):
                    for s in range(2):
                        n = 2 * c + s
                        dve.wait_ge(projected, n + 1 + FIRST)
                        if c:
                            dve.wait_ge(stored[s], c * PARTS * 16)
                        nc.vector.tensor_copy(part[:, s, 0, :], p_qk[:, s, :]).then_inc(first, 1)
                        dve.wait_ge(first, n + 1 + FIRST)
                        nc.vector.tensor_tensor(rest[:, s, 0, :], p_qk[:, s, :], part[:, s, 0, :],
                                                ALU.subtract).then_inc(rest1, 1)
                        dve.wait_ge(rest1, n + 1 + FIRST)
                        nc.vector.tensor_copy(part[:, s, 1, :], rest[:, s, 0, :]).then_inc(second, 1)
                        dve.wait_ge(second, n + 1 + FIRST)
                        nc.vector.tensor_tensor(part[:, s, 2, :], rest[:, s, 0, :], part[:, s, 1, :],
                                                ALU.subtract).then_inc(third, 1)


def attention(nc, A, tag, vals, attn, q_parts, k_parts, ident, causal):
    with ExitStack() as ctx:
        def sb(name, shape, dt=F32):
            return ctx.enter_context(nc.sbuf_tensor(f"{tag}_{name}", shape, dt))

        sem = semaphores(nc, ctx, f"{tag}")

        QS = sb("QS", [P, 2, GH, SEQ], BF16)
        KS = sb("KS", [P, 2, GH, SEQ], BF16)
        KZ = sb("KZ", [P, 2, GH, SEQ], BF16)
        V = [sb(f"V{i}", [P, TPB, GH, 32]) for i in range(2)]
        probs = sb("probs", [P, 2, GH, CH])
        mpart = sb("mpart", [P, GH, TPB, 2])
        mcol = sb("mcol", [P, GH * TPB])
        mrow = sb("mrow", [GH * TPB, 3, P], BF16)
        mrest = sb("mrest", [GH * TPB, P])
        osum = sb("osum", [P, CH])
        rsum = sb("rsum", [P, 4 * GH, 1])
        cmask = sb("cmask", [P, 3, P])
        cmaskb = sb("cmaskb", [P, 3, P], BF16)
        p_s = ctx.enter_context(nc.psum_tensor(f"{tag}_ps", [P, 2, 2, CH], F32))
        p_m = ctx.enter_context(nc.psum_tensor(f"{tag}_pm", [P, 2, CH], F32))
        p_o = ctx.enter_context(nc.psum_tensor(f"{tag}_po", [P, CH], F32))
        p_t = ctx.enter_context(nc.psum_tensor(f"{tag}_pt", [P, 4, GH, 32], F32))

        if causal:
            steps = [(hq, kt, max(0, kt * P - hq * CH)) for hq in range(2) for kt in range(4 * hq + 4)]
            chunks = [(h, qt, kc, min(CH, (qt + 1) * P - kc * CH)) for qt in range(TPB)
                      for h in range(GH) for kc in range(qt * P // CH + 1)]
        else:
            steps = [(hq, kt, 0) for hq in range(2) for kt in range(TPB)]
            chunks = [(h, qt, kc, CH) for qt in range(TPB) for h in range(GH) for kc in range(2)]
        NS, NC = len(steps), len(chunks)
        ends = [s for s in range(NS) if s == NS - 1 or steps[s + 1][0] != steps[s][0]]
        per_step = -(-NC // (NS - 3))

        operands, stage_ready = sem("operands", 0), sem("stage_ready")
        maxima, max_read = sem("maxima"), sem("max_read")
        m_all, m_turned, m_lead, m_left, m_split, m_stored = (
            sem("m_all"), sem("m_turned"), sem("m_lead"), sem("m_left"), sem("m_split"), sem("m_stored", 0))
        scores, exped, weighted = sem("scores"), sem("exped"), sem("weighted")
        o_kept, o_turned, o_inv, o_stored = sem("o_kept"), sem("o_turned"), sem("o_inv"), sem("o_stored")
        v_ready, consts, cast, zeroed = sem("v_ready"), sem("consts", 0), sem("cast"), sem("zeroed")
        m_part2, m_done2 = sem("m_part2"), sem("m_mid")

        with nc.Block() as block:
            @block.sync
            def _(sp):
                sp.dma_start(cmask[:, :, :], A["c_causal"]).then_inc(consts, 16)
                sp.wait_ge(zeroed, 5 + FIRST)
                qg = q_parts.rearrange("(g h d) j t -> g (d j) h t", h=GH, d=HD)
                kg = k_parts.rearrange("(g h d) j t -> g (d j) h t", h=GH, d=HD)

                def load(g, par):
                    for h in range(GH):
                        sp.dma_start(QS[0:KROWS, par, h, :], qg[g, :, h, :]).then_inc(operands, 16)
                        sp.dma_start(KZ[0:KROWS, par, h, :], kg[g, :, h, :]).then_inc(operands, 16)
                        sp.dma_start(KS[0:KROWS, par, h, :], kg[g, :, h, :]).then_inc(operands, 16)

                load(0, 0)
                load(1, 1)
                for g in range(2, GROUPS + 1):
                    sp.wait_ge(scores, 2 * NS * (g - 1) + FIRST)
                    load(g % GROUPS, g % 2)

            @block.gpsimd
            def _(pool):
                nc.gpsimd.memset(KS[:, :, :, :], 0.0).then_inc(zeroed, 1)
                nc.gpsimd.memset(V[0][:, :, :, :], 0.0).then_inc(v_ready, 1)
                nc.gpsimd.memset(V[1][:, :, :, :], 0.0).then_inc(v_ready, 1)
                pool.wait_ge(v_ready, 2 + FIRST)
                with pool.Fori(0, GROUPS // 2) as i:
                    for par in range(2):
                        g = i * 2 + par
                        pool.wait_ge(v_ready, 2 + FIRST)
                        pool.wait_ge(weighted, g * NS + FIRST)
                        src = vals[:, ds(i // 2 * TPB, TPB), ds((i % 2) * 2 * GH + par * GH, GH), :]
                        nc.gpsimd.tensor_copy(V[par][:, :, :, 0:HD + 1], src).then_inc(v_ready, 1)

            @block.vector
            def _(dve):
                nc.vector.memset(QS[:, :, :, :], 0.0).then_inc(zeroed, 1)
                nc.vector.memset(KZ[:, :, :, :], 0.0).then_inc(zeroed, 1)
                nc.vector.memset(mpart[:, :, :, :], NEG).then_inc(zeroed, 1)
                dve.wait_ge(zeroed, 4 + FIRST)
                nc.vector.memset(KS[32:64, :, :, :], -1.0).then_inc(zeroed, 1)
                dve.wait_ge(zeroed, 5 + FIRST)
                dve.wait_ge(consts, 16)
                nc.vector.tensor_copy(cmaskb[:, :, :], cmask[:, :, :]).then_inc(cast, 1)

                def half_max(k, g):
                    h, qt, kc, width = chunks[k]
                    dve.wait_ge(maxima, g * NC + (k + 1) + FIRST)
                    nc.vector.reduce_max(mpart[:, h, qt, kc:kc + 1], p_m[:, k % 2, 0:width],
                                         AX_X).then_inc(max_read, 1)

                def finish_maxima(g):
                    dve.wait_ge(max_read, (g + 1) * NC + FIRST)
                    nc.vector.tensor_reduce(mcol[:, :], mpart[:, :, :, :].rearrange("p h q c -> p (h q) c"),
                                            AX_X, ALU.max).then_inc(m_all, 1)
                    dve.wait_ge(m_turned, g + 1 + FIRST)
                    rows = p_t[0:GH * TPB, :, :, :].rearrange("p a h d -> p (a h d)")[:, 0:P]
                    nc.vector.tensor_copy(mrow[:, 0, :], rows).then_inc(m_lead, 1)
                    dve.wait_ge(m_lead, g + 1 + FIRST)
                    nc.vector.tensor_tensor(mrest[:, :], rows, mrow[:, 0, :], ALU.subtract).then_inc(m_left, 1)
                    dve.wait_ge(m_left, g + 1 + FIRST)
                    nc.vector.tensor_copy(mrow[:, 1, :], mrest[:, :]).then_inc(m_part2, 1)
                    dve.wait_ge(m_part2, g + 1 + FIRST)
                    nc.vector.tensor_tensor(mrow[:, 2, :], mrest[:, :], mrow[:, 1, :],
                                            ALU.subtract).then_inc(m_split, 1)

                def keep_out(g, half):
                    u = g * 2 + half
                    dve.wait_ge(weighted, g * NS + ends[half] + 1 + FIRST)
                    dve.wait_ge(o_turned, u + FIRST)
                    nc.vector.tensor_copy(osum[:, :], p_o[:, :]).then_inc(o_kept, 1)

                def normalise(g, half, pos):
                    u = g * 2 + half
                    dve.wait_ge(o_turned, u + 1 + FIRST)
                    nc.vector.reciprocal(rsum[:, :, :],
                                         p_t[:, :, :, HD:HD + 1].rearrange("p a h o -> p (a h) o")).then_inc(o_inv, 1)
                    dve.wait_ge(o_inv, u + 1 + FIRST)
                    tile, head = pos
                    dst = attn[:, ds(tile + 4 * half, 4), ds(head * HD, GH * HD)]
                    nc.vector.tensor_tensor(
                        dst.rearrange("p a (h d) -> p a h d", h=GH),
                        p_t[:, :, :, 0:HD],
                        rsum[:, :, :].rearrange("p (a h) o -> p a h o", a=4).broadcast_to([P, 4, GH, HD]),
                        ALU.mult).then_inc(o_stored, 1)

                for k in range(NC):
                    half_max(k, 0)
                finish_maxima(0)
                with dve.Fori(0, GROUPS // 2) as i:
                    for par in range(2):
                        g = i * 2 + par
                        pos = (i // 2 * TPB, (i % 2) * 2 * GH + par * GH)
                        k = 0
                        for s in range(NS):
                            if s == ends[0] + 2:
                                keep_out(g, 0)
                            while k < min(NC, (s + 1) * per_step):
                                half_max(k, g + 1)
                                k += 1
                            if s == ends[0] + 2:
                                normalise(g, 0, pos)
                            if s == NS - 3:
                                finish_maxima(g + 1)
                        keep_out(g, 1)
                        normalise(g, 1, pos)

            @block.tensor
            def _(pe):
                pe.wait_ge(cast, 1 + FIRST)

                def max_chunk(k, g, par):
                    h, qt, kc, width = chunks[k]
                    if g is not None:
                        pe.wait_ge(max_read, g * NC + k - 1 + FIRST)
                    elif k >= 2:
                        pe.wait_ge(max_read, k - 1 + FIRST)
                    diag = causal and kc * CH + width == (qt + 1) * P
                    out = p_m[:, k % 2, 0:width]
                    mm = nc.tensor.matmul(out, QS[:, par, h, qt * P:(qt + 1) * P],
                                          KZ[:, par, h, kc * CH:kc * CH + width], start=True, stop=True)
                    if diag:
                        mm = nc.tensor.matmul(p_m[:, k % 2, width - P:width], cmaskb[:, 0, :],
                                              cmaskb[:, 1, :], start=False, stop=True, skip_group_check=True)
                    mm.then_inc(maxima, 1)

                def turn_maxima(g):
                    pe.wait_ge(m_all, g + 1 + FIRST)
                    pe.wait_ge(o_stored, g * 2 - 1 + FIRST)
                    rows = p_t[0:GH * TPB, :, :, :].rearrange("p a h d -> p (a h d)")[:, 0:P]
                    nc.tensor.transpose(rows, mcol[:, :], ident[:, :]).then_inc(m_turned, 1)

                def score(s, g, par, pair):
                    hq, kt, c0 = steps[s]
                    pe.wait_ge(exped, (g * (2 * NS) + (2 * s + pair - 1 if s else 0)) + FIRST)
                    for e in range(2):
                        h = 2 * pair + e
                        q0 = hq * CH + c0
                        diag = causal and kt * P >= hq * CH
                        mm = nc.tensor.matmul(p_s[:, pair, e, c0:CH], KS[:, par, h, kt * P:(kt + 1) * P],
                                              QS[:, par, h, q0:(hq + 1) * CH], start=True, stop=True)
                        if diag:
                            mm = nc.tensor.matmul(p_s[:, pair, e, c0:c0 + P], cmaskb[:, 0, :],
                                                  cmaskb[:, 2, :], start=False, stop=True,
                                                  skip_group_check=True)
                    mm.then_inc(scores, 1)

                def weigh(s, g, par):
                    hq, kt, c0 = steps[s]
                    pe.wait_ge(exped, g * (2 * NS) + 2 * s + 2 + FIRST)
                    if s == 0:
                        pe.wait_ge(v_ready, g + 3 + FIRST)
                    if kt == 0:
                        pe.wait_ge(o_kept, g * 2 + hq + FIRST)
                    for h in range(GH):
                        mm = nc.tensor.matmul(p_o[32 * h:32 * h + 32, c0:CH], V[par][:, kt, h, :],
                                              probs[:, s % 2, h, c0:CH], start=kt == 0, stop=s in ends,
                                              skip_group_check=True)
                    mm.then_inc(weighted, 1)

                def turn_out(u, maxima_before):
                    pe.wait_ge(o_kept, u + 1 + FIRST)
                    pe.wait_ge(m_split, maxima_before + FIRST)
                    pe.wait_ge(o_stored, u + FIRST)
                    for t in range(4):
                        mm = nc.tensor.transpose(p_t[:, t, :, :].rearrange("p h d -> p (h d)"),
                                                 osum[:, t * P:(t + 1) * P], ident[:, :])
                    mm.then_inc(o_turned, 1)

                pe.wait_ge(operands, 2 * 3 * GH * 16)
                for k in range(NC):
                    max_chunk(k, None, 0)
                pe.wait_ge(m_all, 1 + FIRST)
                rows0 = p_t[0:GH * TPB, :, :, :].rearrange("p a h d -> p (a h d)")[:, 0:P]
                nc.tensor.transpose(rows0, mcol[:, :], ident[:, :]).then_inc(m_turned, 1)
                with pe.Fori(0, GROUPS // 2) as i:
                    for par in range(2):
                        g = i * 2 + par
                        pe.wait_ge(m_stored, g * 48 + 48)
                        pe.wait_ge(operands, (g + 2) * (3 * GH * 16))
                        k = 0
                        for s in range(NS):
                            score(s, g, par, 0)
                            first = k
                            while k < min(NC, (s + 1) * per_step):
                                if k == first + 2:
                                    score(s, g, par, 1)
                                max_chunk(k, g + 1, 1 - par)
                                k += 1
                            if k - first <= 2:
                                score(s, g, par, 1)
                            if s == NS - 3:
                                turn_maxima(g + 1)
                            if s:
                                weigh(s - 1, g, par)
                            if s == ends[0] + 2:
                                turn_out(g * 2, g + 1)
                        weigh(NS - 1, g, par)
                        turn_out(g * 2 + 1, g + 2)

            @block.scalar
            def _(act):
                def rows_of(par, g):
                    act.wait_ge(m_split, g + 1 + FIRST)
                    for j in range(3):
                        act.dma_start(QS[KROWS + j:KROWS + j + 1, par, :, :].rearrange("p h t -> p (h t)")
                                      .rearrange("p (r c) -> p r c", c=P),
                                      mrow[:, j, :]).then_inc(m_stored, 16)

                rows_of(0, 0)
                with act.Fori(0, GROUPS // 2) as i:
                    for par in range(2):
                        g = i * 2 + par
                        for s in range(NS):
                            hq, kt, c0 = steps[s]
                            if s == NS - 1:
                                rows_of(1 - par, g + 1)
                            for pair in range(2):
                                act.wait_ge(scores, g * (2 * NS) + 2 * s + pair + 1 + FIRST)
                                if pair == 0:
                                    act.wait_ge(weighted, g * NS + max(s - 1, 0) + FIRST)
                                nc.scalar.activation(probs[:, s % 2, 2 * pair:2 * pair + 2, c0:CH],
                                                     p_s[:, pair, :, c0:CH], ACT.Exp,
                                                     scale=SM_SCALE).then_inc(exped, 1)
                act.wait_ge(m_stored, (GROUPS + 1) * 48)


def finish(nc, A, tag, XT, X0, attn, ident, ones, eps, xin, low_rank):
    with ExitStack() as ctx:
        def sb(name, shape, dt=F32):
            return ctx.enter_context(nc.sbuf_tensor(f"{tag}f_{name}", shape, dt))

        sem = semaphores(nc, ctx, f"{tag}f")

        stage = sb("stage", [P, CH])
        turned = sb("turned", [P, CH])
        low = sb("low", [RANK, CH])
        wdown = sb("wdown", [DIM, RANK])
        wup = sb("wup", [RANK, DIM])
        resid, sq, sd = sb("resid", [P, CH]), sb("sq", [P, CH]), sb("sd", [P, CH])
        p_t = ctx.enter_context(nc.psum_tensor(f"{tag}f_pt", [P, CH], F32))
        p_low = ctx.enter_context(nc.psum_tensor(f"{tag}f_plow", [P, CH], F32))
        p_y = ctx.enter_context(nc.psum_tensor(f"{tag}f_py", [P, CH], F32))
        stat = ctx.enter_context(nc.psum_tensor(f"{tag}f_stat", [P, 2, CH], F32))
        ln = {k: sem(f"ln_{k}") for k in ("resid", "mean", "sq", "var", "sd", "inv", "cent", "out", "kept")}
        weights, staged, t_done, t_kept, low_done, low_kept, y_done = (
            sem("weights", 0), sem("staged"), sem("t_done"), sem("t_kept"), sem("low_done"), sem("low_kept"),
            sem("y_done"))
        with nc.Block() as block:
            if low_rank:
                @block.sync
                def _(sp):
                    sp.dma_start(wdown[:, :], A["o_down"]).then_inc(weights, 16)
                    sp.dma_start(wup[:, :], A["o_up"]).then_inc(weights, 16)

            @block.tensor
            def _(pe):
                if low_rank:
                    pe.wait_ge(weights, 32)
                with pe.Fori(0, CHUNKS) as c:
                    pe.wait_ge(staged, c + 1 + FIRST)
                    pe.wait_ge(ln["resid"], c + FIRST)
                    for t in range(4):
                        mm = nc.tensor.transpose(p_t[:, t * P:(t + 1) * P], stage[:, t * P:(t + 1) * P],
                                                 ident[:, :])
                    mm.then_inc(t_done, 1)
                    if low_rank:
                        pe.wait_ge(t_kept, c + 1 + FIRST)
                        nc.tensor.matmul(p_low[0:RANK, :], wdown[:, :], turned[:, :], start=True,
                                         stop=True).then_inc(low_done, 1)
                        pe.wait_ge(low_kept, c + 1 + FIRST)
                        nc.tensor.matmul(p_y[:, :], wup[:, :], low[:, :], start=True,
                                         stop=True).then_inc(y_done, 1)
                    layer_norm_pe(nc, pe, stat, ones, resid, sq, ln, c)

            @block.scalar
            def _(act):
                with act.Fori(0, CHUNKS) as c:
                    if low_rank:
                        act.wait_ge(t_done, c + 1 + FIRST)
                        nc.scalar.copy(turned[:, :], p_t[:, :]).then_inc(t_kept, 1)
                        act.wait_ge(low_done, c + 1 + FIRST)
                        nc.scalar.copy(low[:, :], p_low[0:RANK, :]).then_inc(low_kept, 1)
                    layer_norm_act(nc, act, stat, sd, eps, ln, c)

            @block.vector
            def _(dve):
                with dve.Fori(0, CHUNKS) as c:
                    dve.wait_ge(t_done, c + FIRST)
                    nc.vector.tensor_copy(stage[:, :],
                                          attn[:, ds(c * 4, 4), :].rearrange("p t d -> p (t d)")).then_inc(staged, 1)
                    dve.wait_ge(y_done if low_rank else t_done, c + 1 + FIRST)
                    dve.wait_ge(ln["out"], c + FIRST)
                    x = XT[:, ds(c * CH + X0, CH)]
                    nc.vector.tensor_tensor(resid[:, :], x, (p_y if low_rank else p_t)[:, :],
                                            ALU.add).then_inc(ln["resid"], 1)
                    layer_norm_dve(nc, dve, stat, resid, sq, sd, x, ln, c,
                                   None if xin is None else xin[:, ds(c * CH, CH)])


def expert_ffn(nc, A, XT, X0, ones, eps):
    WC = 2 * FF + FF // P + 1
    B1, B2 = 2 * FF, 2 * FF + FF // P
    with ExitStack() as ctx:
        def sb(name, shape, dt=F32):
            return ctx.enter_context(nc.sbuf_tensor(f"ffn_{name}", shape, dt))

        sem = semaphores(nc, ctx, "ffn")

        base = sb("base", [P, WC])
        experts = sb("experts", [P, EXPERTS, WC])
        merged = sb("merged", [P, WC])
        gw1 = sb("gw1", [P, DIM])
        gb1 = sb("gb1", [P, 1])
        gw2 = sb("gw2", [P, EXPERTS])
        gb2 = sb("gb2", [P, EXPERTS])
        xb = sb("xb", [P, SEQ])
        hid = sb("hid", [P, CH])
        hsum = sb("hsum", [P, 2])
        hmean = sb("hmean", [P, P])
        htot = sb("htot", [P, 1])
        gate = sb("gate", [P, EXPERTS])
        u = sb("u", [P, 4, CH])
        resid, sq, sd = sb("resid", [P, CH]), sb("sq", [P, CH]), sb("sd", [P, CH])
        p_h = ctx.enter_context(nc.psum_tensor("ffn_ph", [P, CH], F32))
        p_g = ctx.enter_context(nc.psum_tensor("ffn_pg", [P, CH], F32))
        p_u = ctx.enter_context(nc.psum_tensor("ffn_pu", [P, 2, CH], F32))
        p_y = ctx.enter_context(nc.psum_tensor("ffn_py", [P, CH], F32))
        stat = ctx.enter_context(nc.psum_tensor("ffn_stat", [P, 2, CH], F32))
        ln = {k: sem(f"ln_{k}") for k in ("resid", "mean", "sq", "var", "sd", "inv", "cent", "out")}
        weights, x_in, h_done, h_sum, h_tot, h_mean, g_done, gated, merged_s = (
            sem("weights", 0), sem("x_in"), sem("h_done"), sem("h_sum"), sem("h_tot"), sem("h_mean"),
            sem("g_done"), sem("gated"), sem("merged"))
        u_done, u_kept, y_done = sem("u_done"), sem("u_kept"), sem("y_done")
        with nc.Block() as block:
            @block.sync
            def _(sp):
                for dst, name in ((gw1, "gate_w1"), (gb1, "gate_b1"), (gw2, "gate_w2"), (gb2, "gate_b2"),
                                  (base, "ffn_base")):
                    sp.dma_start(dst[:, :], A[name]).then_inc(weights, 16)
                sp.dma_start(experts[:, :, :], A["ffn_experts"]).then_inc(weights, 16)

            @block.tensor
            def _(pe):
                pe.wait_ge(weights, 96)
                with pe.Fori(0, BATCH) as b:
                    for half in range(2):
                        if half:
                            pe.wait_ge(h_sum, b * 2 + 1 + FIRST)
                        else:
                            pe.wait_ge(h_sum, b * 2 + FIRST)
                            pe.wait_ge(x_in, b + 1 + FIRST)
                        nc.tensor.matmul(p_h[:, :], gw1[:, :], xb[:, half * CH:(half + 1) * CH],
                                         start=True, stop=True).then_inc(h_done, 1)
                    pe.wait_ge(h_mean, b + 1 + FIRST)
                    nc.tensor.matmul(p_g[:, 0:EXPERTS], hmean[:, :], gw2[:, :], start=True,
                                     stop=True).then_inc(g_done, 1)
                    pe.wait_ge(merged_s, b * (EXPERTS + 0) + EXPERTS + FIRST)
                    for half in range(2):
                        for f in range(4):
                            back = half * 4 + f - 1
                            if back >= 0:
                                pe.wait_ge(u_kept, b * 8 + back + FIRST)
                            else:
                                pe.wait_ge(u_kept, b * 8 + FIRST)
                            nc.tensor.matmul(p_u[:, f % 2, :], merged[:, f * P:(f + 1) * P],
                                             xb[:, half * CH:(half + 1) * CH], start=True,
                                             stop=True).then_inc(u_done, 1)
                        pe.wait_ge(u_kept, b * 8 + (half * 4 + 4) + FIRST)
                        pe.wait_ge(ln["resid"], b * 2 + half + FIRST)
                        for f in range(4):
                            mm = nc.tensor.matmul(p_y[:, :], merged[:, FF + f * P:FF + (f + 1) * P],
                                                  u[:, f, :], start=f == 0, stop=f == 3)
                        mm.then_inc(y_done, 1)
                        layer_norm_pe(nc, pe, stat, ones, resid, sq, ln, b * 2 + half)

            @block.scalar
            def _(act):
                act.wait_ge(weights, 96)
                with act.Fori(0, BATCH) as b:
                    for half in range(2):
                        act.wait_ge(h_done, b * 2 + (half + 1) + FIRST)
                        act.wait_ge(h_tot, b + FIRST)
                        act.wait_ge(h_sum, b * 2 + half + FIRST)
                        nc.scalar.activation(hid[:, :], p_h[:, :], ACT.Relu, bias=gb1[:, 0:1],
                                             accum_out=hsum[:, half:half + 1]).then_inc(h_sum, 1)
                    for half in range(2):
                        for f in range(4):
                            act.wait_ge(u_done, b * 8 + (half * 4 + f + 1) + FIRST)
                            act.wait_ge(y_done, b * 2 + half + FIRST)
                            nc.scalar.activation(u[:, f, :], p_u[:, f % 2, :], ACT.Gelu_apprx_tanh,
                                                 bias=merged[:, B1 + f:B1 + f + 1]).then_inc(u_kept, 1)
                        layer_norm_act(nc, act, stat, sd, eps, ln, b * 2 + half)

            @block.vector
            def _(dve):
                dve.wait_ge(weights, 96)
                with dve.Fori(0, BATCH) as b:
                    dve.wait_ge(u_done, b * 8 + FIRST)
                    nc.vector.tensor_copy(xb[:, :], XT[:, ds(b * SEQ + X0, SEQ)]).then_inc(x_in, 1)
                    dve.wait_ge(h_sum, b * 2 + 2 + FIRST)
                    nc.vector.reduce_sum(htot[:, :], hsum[:, :], AX_X).then_inc(h_tot, 1)
                    dve.wait_ge(h_tot, b + 1 + FIRST)
                    nc.vector.tensor_scalar(hmean[:, :], ones[:, :], htot[:, 0:1], float(DIM) / SEQ, ALU.mult,
                                            ALU.mult).then_inc(h_mean, 1)
                    dve.wait_ge(g_done, b + 1 + FIRST)
                    nc.vector.tensor_tensor(gate[:, :], p_g[:, 0:EXPERTS], gb2[:, :], ALU.add).then_inc(gated, 1)
                    dve.wait_ge(gated, b + 1 + FIRST)
                    dve.wait_ge(ln["out"], b * 2 + FIRST)
                    for e in range(EXPERTS):
                        if e:
                            dve.wait_ge(merged_s, b * EXPERTS + e + FIRST)
                        nc.vector.scalar_tensor_tensor(
                            merged[:, :], experts[:, e, :], gate[:, e:e + 1],
                            (base if e == 0 else merged)[:, :], ALU.mult, ALU.add).then_inc(merged_s, 1)
                    for half in range(2):
                        dve.wait_ge(y_done, b * 2 + (half + 1) + FIRST)
                        dve.wait_ge(ln["out"], b * 2 + half + FIRST)
                        nc.vector.scalar_tensor_tensor(
                            resid[:, :], p_y[:, :], merged[:, B2:B2 + 1], xb[:, half * CH:(half + 1) * CH],
                            ALU.add, ALU.add).then_inc(ln["resid"], 1)
                        layer_norm_dve(nc, dve, stat, resid, sq, sd, XT[:, ds(b * SEQ + (X0 + half * CH), CH)],
                                       ln, b * 2 + half)


def windowed(nc, A, XT, ident, ones, eps):
    STEPS = TILES + PADL
    KCH = [(0, P), (P, 2 * P), (2 * P, DI)]
    with ExitStack() as ctx:
        def sb(name, shape, dt=F32):
            return ctx.enter_context(nc.sbuf_tensor(f"w_{name}", shape, dt))

        sem = semaphores(nc, ctx, "w")

        def ps(name, shape):
            return ctx.enter_context(nc.psum_tensor(f"w_{name}", shape, F32))

        wqkv = sb("wqkv", [P, 2, 3 * INNER])
        wo = sb("wo", [P, INNER // P, DIM])
        w1 = sb("w1", [P, 2 * DI])
        w2 = sb("w2", [P, 3, DIM])
        vecs = sb("vecs", [P, 10])
        scales = sb("scales", [P, 4, DH])
        rot = sb("rot", [P, 4, TPB, DH])
        tab = sb("tab", [P, 4, TPB, DH])
        wmask = sb("wmask", [P, TPB, 2 * WIN])
        notfirst = sb("notfirst", [P, TPB])

        xs = sb("xs", [P, P])
        xsv = sb("xsv", [P, P])
        sq = sb("sq", [P, 2, CH])
        qk = sb("qk", [P, 2, HEADS, DH])
        qn = sb("qn", [P, 2, HEADS, DH])
        nrm = sb("nrm", [P, 2 * HEADS])
        rn0 = sb("rn0", [P, 2 * HEADS])
        rnh = sb("rnh", [P, 2 * HEADS])
        rn = sb("rn", [P, 2 * HEADS])
        t1 = sb("t1", [P, 2, HEADS, DH])
        t2 = sb("t2", [P, 2, HEADS, DH])
        qT = sb("qT", [P, HEADS // 2, P])
        kT = sb("kT", [P, HEADS // 2, WIN + P])
        vt = sb("vt", [P, INNER])
        v0 = sb("v0", [P, INNER])
        sm = sb("sm", [P, HEADS, 2 * WIN])
        mx = sb("mx", [P, HEADS])
        den = sb("den", [P, HEADS])
        pd = sb("pd", [P, HEADS, P])
        pT = sb("pT", [P, HEADS, P])
        oT = sb("oT", [P, HEADS // 2, P])
        x1 = sb("x1", [P, P + 1])
        xs2 = sb("xs2", [P, P])
        sq2 = sb("sq2", [P, P])
        rs0 = sb("rs0", [P, P])
        rsh = sb("rsh", [P, P])
        gl = sb("gl", [P, 3, P])
        hid = sb("hid", [P, 3, P])

        b_proj = [ps(f"proj{j}", [P, CH]) for j in range(2)]
        b_s = [ps(f"s{j}", [P, HEADS // 2, 2 * WIN]) for j in range(2)]
        b_t = [ps(f"tb{j}", [P, 4, P]) for j in range(2)]
        b_o = ps("o", [P, 4, P])
        b_c = ps("c", [P, 3, P])

        TURNS = ("q", "k", "p", "pp", "ffn")
        S = {k: sem(k, 0 if k in ("consts", "proj_weights", "out_weights") else FIRST) for k in (
            "consts", "proj_weights", "out_weights", "cleared", "tables", "xs", "xsv", "k_prev", "scored0",
            "scored1", "masked0", "masked1", "mx", "shifted", "exped", "den", "rden", "scaled", "spread",
            "summed0", "summed1", "o_kept0", "o_kept1", "v_prev", "y", "x1", "x1p", "xs2", "mean", "cent",
            "sq2", "var", "lnv", "rs0", "rsv", "rsh", "xr", "xn1", "xn", "out", "x2", "nmax", "lnn", "rn0",
            "rna", "rnh", "rn", "scaled_q", "scaled_k", "cosq", "cosk", "sinq", "sink", "rotq", "rotk",
            *(f"proj{c}" for c in range(6)), *(f"kept{c}" for c in range(6)),
            *(f"squared{c}" for c in range(4)), *(f"normed{c}" for c in range(4)),
            *(f"turn{j}_{w}" for j in range(2) for w in TURNS),
            *(f"free{j}_{w}" for j in range(2) for w in TURNS))}

        with nc.Block() as block:
            @block.sync
            def _(sp):
                sp.dma_start(rot[:, :, :, :], A["c_rot"]).then_inc(S["consts"], 16)
                sp.dma_start(wmask[:, :, :], A["c_wmask"]).then_inc(S["consts"], 16)
                sp.dma_start(notfirst[:, :], A["c_notfirst"]).then_inc(S["consts"], 16)
                for l in range(DEPTH):
                    if l:
                        sp.wait_ge(S["tables"], l + FIRST)
                        sp.wait_ge(S["proj_weights"], 32 * l)
                    if l >= 2:
                        sp.wait_ge(S["proj5"], (l - 1) * STEPS + FIRST)
                    sp.dma_start(wqkv[:, l % 2, :], A["w_qkv"][l]).then_inc(S["proj_weights"], 16)
                    sp.dma_start(scales[:, :, :], A["w_scales"][l]).then_inc(S["proj_weights"], 16)
                    if l:
                        sp.wait_ge(S["x2"], l * STEPS + FIRST)
                    sp.dma_start(wo[:, :, :], A["w_o"][l]).then_inc(S["out_weights"], 16)
                    sp.dma_start(w1[:, :], A["w_1"][l]).then_inc(S["out_weights"], 16)
                    sp.dma_start(w2[:, :, :], A["w_2"][l]).then_inc(S["out_weights"], 16)
                    sp.dma_start(vecs[:, :], A["w_vecs"][l]).then_inc(S["out_weights"], 16)

            @block.gpsimd
            def _(pool):
                for tile in (qT, kT, sm, pd, oT, pT):
                    ms = nc.gpsimd.memset(tile[:, :, :], 0.0)
                for tile in (vt, v0, x1):
                    ms = nc.gpsimd.memset(tile[:, :], 0.0)
                nc.gpsimd.memset(t2[:, 0, :, :], 0.0)
                ms = nc.gpsimd.memset(t1[:, :, :, :], 0.0)
                ms.then_inc(S["cleared"], 1)
                with pool.Fori(0, DEPTH) as l:
                    with pool.Fori(0, STEPS) as i:
                        n = l * STEPS + i
                        pool.wait_ge(S["scaled_k"], n + 1 + FIRST)
                        for half in range(2):
                            dst = slice(half * 32, half * 32 + 32)
                            src = slice(32 - half * 32, 64 - half * 32)
                            op = nc.gpsimd.tensor_tensor(
                                t2[:, 1, :, dst], qn[:, 1, :, src],
                                tab[:, 3, ds(i % TPB, 1), dst].broadcast_to([P, HEADS, 32]), ALU.mult)
                        op.then_inc(S["sink"], 1)
                        pool.wait_ge(S["turn0_k"], n + 1 + FIRST)
                        pool.wait_ge(S["turn1_k"], n + 1 + FIRST)
                        nc.gpsimd.tensor_tensor(
                            t1[:, 1, :, :], qn[:, 1, :, :],
                            tab[:, 2, ds(i % TPB, 1), :].broadcast_to([P, HEADS, DH]),
                            ALU.mult).then_inc(S["cosk"], 1)
                        pool.wait_ge(S["sink"], n + 1 + FIRST)
                        pool.wait_ge(S["cosk"], n + 1 + FIRST)
                        nc.gpsimd.tensor_tensor(t1[:, 1, :, :], t1[:, 1, :, :], t2[:, 1, :, :],
                                                ALU.add).then_inc(S["rotk"], 1)
                        pool.wait_ge(S["rden"], n + 1 + FIRST)
                        nc.gpsimd.tensor_tensor(
                            sm[:, :, :], sm[:, :, :], den[:, :].unsqueeze(2).broadcast_to([P, HEADS, 2 * WIN]),
                            ALU.mult).then_inc(S["scaled"], 1)

            @block.tensor
            def _(pe):
                pe.wait_ge(S["cleared"], 1 + FIRST)
                with pe.Fori(0, DEPTH) as l:
                    with pe.Fori(0, STEPS) as i:
                        n = l * STEPS + i

                        def proj(c):
                            if c < 2:
                                pe.wait_ge(S[f"kept{c + 4}"], n + FIRST)
                            else:
                                pe.wait_ge(S[f"kept{c - 2}"], n + 1 + FIRST)
                            if c == 0:
                                pe.wait_ge(S["xs"], n + 1 + FIRST)
                            if c == 4:
                                pe.wait_ge(S["xsv"], n + 1 + FIRST)
                            nc.tensor.matmul(b_proj[c % 2][:, :], (xs if c < 4 else xsv)[:, :],
                                             wqkv[:, ds(l % 2, 1), c * CH:(c + 1) * CH].rearrange("p a f -> p (a f)"),
                                             start=True, stop=True).then_inc(S[f"proj{c}"], 1)

                        def bank_free(j, what):
                            before = TURNS.index(what) - 1
                            pe.wait_ge(S[f"free{j}_{TURNS[before]}"], (n if before < 0 else n + 1) + FIRST)

                        def turn_qk(a):
                            what = TURNS[a]
                            if a == 0:
                                pe.wait_ge(S["rotq"], n + 1 + FIRST)
                            else:
                                pe.wait_ge(S["rotk"], n + FIRST)
                            src = t1[:, a, :, :].rearrange("p h d -> p (h d)")
                            for j in range(2):
                                bank_free(j, what)
                                for k in range(4):
                                    c0 = (4 * j + k) * P
                                    mm = nc.tensor.transpose(b_t[j][:, k, :], src[:, c0:c0 + P], ident[:, :])
                                mm.then_inc(S[f"turn{j}_{what}"], 1)

                        def turn_p(grp):
                            j, what = grp % 2, ("p", "pp")[grp // 2]
                            if grp == 0:
                                pe.wait_ge(S["spread"], n + 1 + FIRST)
                            bank_free(j, what)
                            for k in range(4):
                                mm = nc.tensor.transpose(b_t[j][:, k, :], pd[:, 4 * grp + k, :], ident[:, :])
                            mm.then_inc(S[f"turn{j}_{what}"], 1)

                        def values(half):
                            if half == 0:
                                for what in ("v_prev", "kept4", "kept5", "free0_pp", "free1_pp"):
                                    pe.wait_ge(S[what], n + 1 + FIRST)
                                pe.wait_ge(S["x1"], n + 1 + FIRST)
                            else:
                                pe.wait_ge(S["o_kept0"], n + 1 + FIRST)
                            for k in range(4):
                                p = 4 * half + k
                                for cols, val in ((slice(WIN, P), vt), (slice(0, WIN), v0)):
                                    for e in range(2):
                                        f = (2 * p + e) * DH
                                        mm = nc.tensor.matmul(b_o[64 * e:64 * e + 64, k, cols],
                                                              val[:, f:f + DH],
                                                              pT[:, e * 8 + p, cols],
                                                              start=True, stop=True)
                            mm.then_inc(S[f"summed{half}"], 1)

                        pe.wait_ge(S["out_weights"], l * 64 + 64)
                        pe.wait_ge(S["o_kept1"], n + FIRST)
                        for p in range(HEADS // 2):
                            mm = nc.tensor.matmul(b_o[:, 0, :], wo[:, p, :], oT[:, p, :], start=p == 0,
                                                  stop=p == HEADS // 2 - 1)
                        mm.then_inc(S["y"], 1)
                        pe.wait_ge(S["proj_weights"], l * 32 + 32)
                        proj(0)
                        turn_qk(0)
                        pe.wait_ge(S["x2"], n + FIRST)
                        pe.wait_ge(S["xs2"], n + 1 + FIRST)
                        nc.tensor.matmul(b_c[:, 0, :], ones[:, :], xs2[:, :], start=True,
                                         stop=True).then_inc(S["mean"], 1)
                        proj(1)
                        turn_qk(1)
                        proj(2)
                        pe.wait_ge(S["free0_k"], n + 1 + FIRST)
                        pe.wait_ge(S["free1_k"], n + 1 + FIRST)
                        pe.wait_ge(S["masked0"], n + FIRST)
                        pe.wait_ge(S["masked1"], n + FIRST)
                        pe.wait_ge(S["sq2"], n + 1 + FIRST)
                        nc.tensor.matmul(b_c[:, 1, :], ones[:, :], sq2[:, :], start=True,
                                         stop=True).then_inc(S["var"], 1)
                        proj(3)
                        for p in range(HEADS // 2):
                            for e in range(2):
                                r = slice(64 * e, 64 * e + 64)
                                for w in range(4):
                                    mm = nc.tensor.matmul(
                                        b_s[e][32 * w:32 * w + 32, p, :], qT[r, p, 32 * w:32 * w + 32],
                                        kT[r, p, 32 * w:32 * w + 64], start=True, stop=True)
                                if p == HEADS // 2 - 1:
                                    mm.then_inc(S[f"scored{e}"], 1)
                        turn_p(0)
                        turn_p(1)
                        proj(4)
                        turn_p(2)
                        turn_p(3)
                        proj(5)
                        pe.wait_ge(S["xn"], n + 1 + FIRST)
                        for j, off in ((0, DI), (1, 0)):
                            bank_free(j, "ffn")
                            for k, (lo, hi) in enumerate(KCH):
                                mm = nc.tensor.matmul(b_t[j][0:hi - lo, k, :], w1[:, off + lo:off + hi],
                                                      xs2[:, :], start=True, stop=True)
                            mm.then_inc(S[f"turn{j}_ffn"], 1)
                        values(0)
                        values(1)
                        pe.wait_ge(S["free1_ffn"], n + 1 + FIRST)
                        for k, (lo, hi) in enumerate(KCH):
                            mm = nc.tensor.matmul(b_c[:, 2, :], w2[0:hi - lo, k, :], hid[0:hi - lo, k, :],
                                                  start=k == 0, stop=k == 2)
                        mm.then_inc(S["out"], 1)

            @block.scalar
            def _(act):
                act.wait_ge(S["cleared"], 1 + FIRST)
                nc.scalar.preload_act_table_set("natural_log_exp_and_others")
                with act.Fori(0, DEPTH) as l:
                    act.wait_ge(S["out_weights"], l * 64 + 64)
                    with act.Fori(0, STEPS) as i:
                        n = l * STEPS + i

                        def keep(c):
                            act.wait_ge(S[f"proj{c}"], n + 1 + FIRST)
                            if c == 0:
                                act.wait_ge(S["scaled_q"], n + FIRST)
                            if c < 2:
                                act.wait_ge(S[f"normed{c + 2}"], n + FIRST)
                            else:
                                act.wait_ge(S[f"normed{c - 2}"], n + 1 + FIRST)
                            nc.scalar.square(sq[:, c % 2, :], b_proj[c % 2][:, :]).then_inc(S[f"squared{c}"], 1)
                            nc.scalar.copy(qk[:, c // 2, 8 * (c % 2):8 * (c % 2) + 8, :].rearrange("p h d -> p (h d)"),
                                           b_proj[c % 2][:, :]).then_inc(S[f"kept{c}"], 1)

                        def turned(what, dst):
                            act.wait_ge(S[f"turn0_{what}"], n + 1 + FIRST)
                            nc.scalar.copy(dst, b_t[0][:, :, :]).then_inc(S[f"free0_{what}"], 1)

                        def spread(windows):
                            for w in windows:
                                r = slice(32 * w, 32 * w + 32)
                                if w == 0:
                                    act.wait_ge(S["scaled"], n + FIRST)
                                    act.wait_ge(S["turn0_pp"], n + FIRST)
                                    act.wait_ge(S["turn1_pp"], n + FIRST)
                                    nc.scalar.copy(pd[r, :, 96:128], sm[r, :, 0:32])
                                    nc.scalar.copy(pd[r, :, 0:32], sm[r, :, 32:64])
                                else:
                                    op = nc.scalar.copy(pd[r, :, 32 * w - 32:32 * w + 32], sm[r, :, :])
                                if w == 3:
                                    op.then_inc(S["spread"], 1)

                        def o_kept(half):
                            if half == 0:
                                act.wait_ge(S["y"], n + 1 + FIRST)
                            act.wait_ge(S[f"summed{half}"], n + 1 + FIRST)
                            nc.scalar.copy(oT[:, 4 * half:4 * half + 4, :],
                                           b_o[:, :, :]).then_inc(S[f"o_kept{half}"], 1)

                        act.wait_ge(S["scored0"], n + FIRST)
                        act.wait_ge(S["scored1"], n + FIRST)
                        nc.scalar.copy(kT[:, :, 0:WIN], kT[:, :, P:P + WIN]).then_inc(S["k_prev"], 1)
                        act.wait_ge(S["summed1"], n + FIRST)
                        nc.scalar.copy(v0[96:128, :], vt[96:128, :]).then_inc(S["v_prev"], 1)
                        keep(0)
                        turned("q", qT[:, 0:4, :])
                        spread((0,))
                        keep(1)
                        act.wait_ge(S["k_prev"], n + 1 + FIRST)
                        turned("k", kT[:, 0:4, WIN:WIN + P])
                        keep(2)
                        act.wait_ge(S["var"], n + 1 + FIRST)
                        nc.scalar.activation(rs0[:, :], b_c[:, 1, :], ACT.Ln, bias=eps[:, 0:1]).then_inc(S["lnv"], 1)
                        act.wait_ge(S["lnv"], n + 1 + FIRST)
                        nc.scalar.activation(rs0[:, :], rs0[:, :], ACT.Exp, scale=-0.5).then_inc(S["rs0"], 1)
                        spread((1, 2, 3))
                        keep(3)
                        act.wait_ge(S["nmax"], n + 1 + FIRST)
                        nc.scalar.activation(rn0[:, :], nrm[:, :], ACT.Ln).then_inc(S["lnn"], 1)
                        act.wait_ge(S["lnn"], n + 1 + FIRST)
                        nc.scalar.activation(rn0[:, :], rn0[:, :], ACT.Exp, scale=-0.5).then_inc(S["rn0"], 1)
                        turned("p", pT[:, 0:4, :])
                        turned("pp", pT[:, 8:12, :])
                        for c in (4, 5):
                            cols = slice((c - 4) * CH, (c - 3) * CH)
                            act.wait_ge(S[f"proj{c}"], n + 1 + FIRST)
                            nc.scalar.copy(v0[0:WIN, cols], b_proj[c % 2][0:WIN, :])
                            nc.scalar.copy(vt[:, cols], b_proj[c % 2][:, :]).then_inc(S[f"kept{c}"], 1)
                        act.wait_ge(S["shifted"], n + 1 + FIRST)
                        nc.scalar.activation(sm[:, :, :], sm[:, :, :], ACT.Exp).then_inc(S["exped"], 1)
                        nc.scalar.preload_act_table(ACT.Gelu)
                        o_kept(0)
                        act.wait_ge(S["turn0_ffn"], n + 1 + FIRST)
                        act.wait_ge(S["free1_ffn"], n + FIRST)
                        for k, (lo, hi) in enumerate(KCH):
                            op = nc.scalar.activation(gl[0:hi - lo, k, :], b_t[0][0:hi - lo, k, :], ACT.Gelu,
                                                      bias=vecs[0:hi - lo, 7 + k:8 + k])
                        op.then_inc(S["free0_ffn"], 1)
                        o_kept(1)
                        nc.scalar.preload_act_table_set("natural_log_exp_and_others")

            @block.vector
            def _(dve):
                dve.wait_ge(S["consts"], 48)
                dve.wait_ge(S["cleared"], 1 + FIRST)
                with dve.Fori(0, DEPTH) as l:
                    dve.wait_ge(S["proj_weights"], l * 32 + 32)
                    dve.wait_ge(S["out_weights"], l * 64 + 64)
                    dve.wait_ge(S["rotk"], l * STEPS + FIRST)
                    for j in range(4):
                        op = nc.vector.tensor_tensor(
                            tab[:, j, :, :], rot[:, j, :, :],
                            scales[:, j:j + 1, :].broadcast_to([P, TPB, DH]), ALU.mult)
                    op.then_inc(S["tables"], 1)
                    with dve.Fori(0, STEPS) as i:
                        n = l * STEPS + i

                        def shifted_tile(dst, lag, done):
                            col = (PADL - lag) * P
                            nc.vector.tensor_copy(dst[0:64, :], XT[0:64, ds(i * P + col, P)])
                            nc.vector.tensor_copy(dst[64:128, 1:P], XT[64:128, ds(i * P + col, P - 1)])
                            nc.vector.tensor_tensor(dst[64:128, 0:1], XT[64:128, ds(i * P + (col - 1), 1)],
                                                    notfirst[64:128, ds((i + TPB - lag) % TPB, 1)],
                                                    ALU.mult).then_inc(S[done], 1)

                        def norms(c):
                            dve.wait_ge(S[f"squared{c}"], n + 1 + FIRST)
                            nc.vector.reduce_sum(nrm[:, 8 * c:8 * c + 8],
                                                 sq[:, c % 2, :].rearrange("p (h d) -> p h d", h=8),
                                                 AX_X).then_inc(S[f"normed{c}"], 1)

                        def turned(what, dst):
                            dve.wait_ge(S[f"turn1_{what}"], n + 1 + FIRST)
                            nc.vector.tensor_copy(dst, b_t[1][:, :, :]).then_inc(S[f"free1_{what}"], 1)

                        dve.wait_ge(S["tables"], l + 1 + FIRST)
                        dve.wait_ge(S["proj3"], n + FIRST)
                        dve.wait_ge(S["x2"], n + FIRST)
                        shifted_tile(xs, 0, "xs")
                        dve.wait_ge(S["cosq"], n + FIRST)
                        dve.wait_ge(S["sinq"], n + FIRST)
                        nc.vector.tensor_tensor(t1[:, 0, :, :], t1[:, 0, :, :], t2[:, 0, :, :],
                                                ALU.add).then_inc(S["rotq"], 1)
                        nc.vector.tensor_tensor(x1[64:128, 0:1], x1[64:128, P:P + 1],
                                                notfirst[64:128, ds((i + TPB - 3) % TPB, 1)],
                                                ALU.mult).then_inc(S["x1p"], 1)
                        dve.wait_ge(S["y"], n + 1 + FIRST)
                        dve.wait_ge(S["x1p"], n + 1 + FIRST)
                        nc.vector.tensor_tensor(x1[:, 1:P + 1], XT[:, ds(i * P, P)], b_o[:, 0, :],
                                                ALU.add).then_inc(S["x1"], 1)
                        dve.wait_ge(S["x1"], n + 1 + FIRST)
                        nc.vector.tensor_copy(xs2[0:64, :], x1[0:64, 1:P + 1])
                        nc.vector.tensor_copy(xs2[64:128, :], x1[64:128, 0:P]).then_inc(S["xs2"], 1)
                        turned("q", qT[:, 4:8, :])
                        dve.wait_ge(S["mean"], n + 1 + FIRST)
                        nc.vector.tensor_tensor(xs2[:, :], xs2[:, :], b_c[:, 0, :], ALU.subtract).then_inc(S["cent"], 1)
                        dve.wait_ge(S["cent"], n + 1 + FIRST)
                        nc.vector.tensor_tensor(sq2[:, :], xs2[:, :], xs2[:, :], ALU.mult).then_inc(S["sq2"], 1)
                        dve.wait_ge(S["k_prev"], n + 1 + FIRST)
                        turned("k", kT[:, 4:8, WIN:WIN + P])
                        norms(0)
                        dve.wait_ge(S["proj5"], n + FIRST)
                        shifted_tile(xsv, 2, "xsv")
                        norms(1)
                        dve.wait_ge(S["rs0"], n + 1 + FIRST)
                        nc.vector.scalar_tensor_tensor(rsh[:, :], b_c[:, 1, :], eps[:, 0:1], rs0[:, :], ALU.add,
                                                       ALU.mult).then_inc(S["rsv"], 1)
                        nc.vector.tensor_tensor(xs2[:, :], xs2[:, :], rs0[:, :], ALU.mult).then_inc(S["xr"], 1)
                        dve.wait_ge(S["rsv"], n + 1 + FIRST)
                        nc.vector.scalar_tensor_tensor(rsh[:, :], rsh[:, :], -0.5, rs0[:, :], ALU.mult,
                                                       ALU.mult).then_inc(S["rsh"], 1)
                        dve.wait_ge(S["xr"], n + 1 + FIRST)
                        dve.wait_ge(S["rsh"], n + 1 + FIRST)
                        nc.vector.scalar_tensor_tensor(xs2[:, :], rsh[:, :], 1.5, xs2[:, :], ALU.add,
                                                       ALU.mult).then_inc(S["xn1"], 1)
                        dve.wait_ge(S["xn1"], n + 1 + FIRST)
                        nc.vector.tensor_scalar(xs2[:, :], xs2[:, :], vecs[:, 0:1], vecs[:, 1:2], ALU.mult,
                                                ALU.add).then_inc(S["xn"], 1)
                        norms(2)
                        norms(3)
                        for c in range(4):
                            dve.wait_ge(S[f"normed{c}"], n + 1 + FIRST)
                        nc.vector.tensor_scalar(nrm[:, :], nrm[:, :], 1e-24, None, ALU.max).then_inc(S["nmax"], 1)
                        for e in range(2):
                            dve.wait_ge(S[f"scored{e}"], n + 1 + FIRST)
                            if e == 0:
                                dve.wait_ge(S["spread"], n + 1 + FIRST)
                            nc.vector.tensor_tensor(
                                sm[:, 8 * e:8 * e + 8, :], b_s[e][:, :, :],
                                wmask[:, ds((i + 7) % TPB, 1), :].broadcast_to([P, 8, 2 * WIN]),
                                ALU.add).then_inc(S[f"masked{e}"], 1)
                        dve.wait_ge(S["summed1"], n + FIRST)
                        turned("p", pT[:, 4:8, :])
                        dve.wait_ge(S["masked0"], n + 1 + FIRST)
                        dve.wait_ge(S["masked1"], n + 1 + FIRST)
                        nc.vector.reduce_max(mx[:, :], sm[:, :, :], AX_X).then_inc(S["mx"], 1)
                        turned("pp", pT[:, 12:16, :])
                        dve.wait_ge(S["mx"], n + 1 + FIRST)
                        nc.vector.tensor_tensor(
                            sm[:, :, :], sm[:, :, :], mx[:, :].unsqueeze(2).broadcast_to([P, HEADS, 2 * WIN]),
                            ALU.subtract).then_inc(S["shifted"], 1)
                        dve.wait_ge(S["rn0"], n + 1 + FIRST)
                        nc.vector.tensor_tensor(rnh[:, :], nrm[:, :], rn0[:, :], ALU.mult).then_inc(S["rna"], 1)
                        dve.wait_ge(S["rna"], n + 1 + FIRST)
                        nc.vector.scalar_tensor_tensor(rnh[:, :], rnh[:, :], -0.5, rn0[:, :], ALU.mult,
                                                       ALU.mult).then_inc(S["rnh"], 1)
                        dve.wait_ge(S["rnh"], n + 1 + FIRST)
                        nc.vector.scalar_tensor_tensor(rn[:, :], rnh[:, :], 1.5, rn0[:, :], ALU.add,
                                                       ALU.mult).then_inc(S["rn"], 1)
                        dve.wait_ge(S["rn"], n + 1 + FIRST)
                        dve.wait_ge(S["kept3"], n + 1 + FIRST)
                        dve.wait_ge(S["rotk"], n + FIRST)
                        for a in (1, 0):
                            nc.vector.tensor_tensor(
                                qn[:, a, :, :], qk[:, a, :, :],
                                rn[:, HEADS * a:HEADS * (a + 1)].unsqueeze(2).broadcast_to([P, HEADS, DH]),
                                ALU.mult).then_inc(S[("scaled_q", "scaled_k")[a]], 1)
                        dve.wait_ge(S["exped"], n + 1 + FIRST)
                        nc.vector.reduce_sum(den[:, :], sm[:, :, :], AX_X).then_inc(S["den"], 1)
                        dve.wait_ge(S["den"], n + 1 + FIRST)
                        nc.vector.reciprocal(den[:, :], den[:, :]).then_inc(S["rden"], 1)
                        dve.wait_ge(S["turn1_ffn"], n + 1 + FIRST)
                        dve.wait_ge(S["free0_ffn"], n + 1 + FIRST)
                        for k, (lo, hi) in enumerate(KCH):
                            op = nc.vector.scalar_tensor_tensor(
                                hid[0:hi - lo, k, :], b_t[1][0:hi - lo, k, :], vecs[0:hi - lo, 4 + k:5 + k],
                                gl[0:hi - lo, k, :], ALU.add, ALU.mult)
                        op.then_inc(S["free1_ffn"], 1)
                        dve.wait_ge(S["scaled_q"], n + 1 + FIRST)
                        for half in range(2):
                            dst = slice(half * 32, half * 32 + 32)
                            src = slice(32 - half * 32, 64 - half * 32)
                            op = nc.vector.tensor_tensor(
                                t2[:, 0, :, dst], qn[:, 0, :, src],
                                tab[:, 1, ds(i % TPB, 1), dst].broadcast_to([P, HEADS, 32]), ALU.mult)
                        op.then_inc(S["sinq"], 1)
                        dve.wait_ge(S["turn0_q"], n + 1 + FIRST)
                        dve.wait_ge(S["turn1_q"], n + 1 + FIRST)
                        nc.vector.tensor_tensor(
                            t1[:, 0, :, :], qn[:, 0, :, :],
                            tab[:, 0, ds(i % TPB, 1), :].broadcast_to([P, HEADS, DH]),
                            ALU.mult).then_inc(S["cosq"], 1)
                        dve.wait_ge(S["out"], n + 1 + FIRST)
                        nc.vector.scalar_tensor_tensor(
                            XT[:, ds(i * P, P)], b_c[:, 2, :], vecs[:, 2:3], x1[:, 1:P + 1], ALU.add,
                            ALU.add).then_inc(S["x2"], 1)


def last_norm(nc, XT, X0, xin, ones, eps, out_dram):
    with ExitStack() as ctx:
        def sb(name, shape, dt=F32):
            return ctx.enter_context(nc.sbuf_tensor(f"last_{name}", shape, dt))

        sem = semaphores(nc, ctx, "last")
        resid, sq, sd = sb("resid", [P, CH]), sb("sq", [P, CH]), sb("sd", [P, CH])
        stat = ctx.enter_context(nc.psum_tensor("last_stat", [P, 2, CH], F32))
        ln = {k: sem(f"ln_{k}") for k in ("resid", "mean", "sq", "var", "sd", "inv", "cent", "out")}
        stored = sem("stored", 0)
        with nc.Block() as block:
            @block.sync
            def _(sp):
                for c in range(CHUNKS):
                    sp.wait_ge(ln["out"], c + 1 + FIRST)
                    sp.dma_start(out_dram[:, c * CH:(c + 1) * CH],
                                 xin[:, c * CH:(c + 1) * CH]).then_inc(stored, 16)
                sp.wait_ge(stored, CHUNKS * 16)

            @block.tensor
            def _(pe):
                with pe.Fori(0, CHUNKS) as c:
                    layer_norm_pe(nc, pe, stat, ones, resid, sq, ln, c)

            @block.scalar
            def _(act):
                with act.Fori(0, CHUNKS) as c:
                    layer_norm_act(nc, act, stat, sd, eps, ln, c)

            @block.vector
            def _(dve):
                with dve.Fori(0, CHUNKS) as c:
                    dve.wait_ge(ln["out"], c + FIRST)
                    nc.vector.tensor_tensor(resid[:, :], XT[:, ds(c * CH + X0, CH)],
                                            xin[:, ds(c * CH, CH)], ALU.add).then_inc(ln["resid"], 1)
                    layer_norm_dve(nc, dve, stat, resid, sq, sd, xin[:, ds(c * CH, CH)], ln, c)


def shape_constants():
    f32 = np.float32
    ident = np.eye(P, dtype=f32)
    k, q = np.arange(P)[:, None], np.arange(P)[None, :]
    causal = np.stack([ident, np.where(q > k, f32(NEG), f32(0)), np.where(k > q, f32(NEG), f32(0))], 1).astype(f32)
    r = np.arange(P) % WIN
    c = np.arange(WIN)
    before = np.where(c[None, :] < r[:, None], f32(NEG), f32(0))
    own = np.where(c[None, :] > r[:, None], f32(NEG), f32(0))
    wmask = np.repeat(np.concatenate([before, own], 1)[:, None, :], TPB, 1).astype(f32)
    wmask[0:WIN, 0, 0:WIN] = NEG
    notfirst = np.ones((P, TPB), f32)
    notfirst[:, 0] = 0
    half = np.arange(0, DH, 2, dtype=f32)
    inv_freq = (f32(1.0) / f32(10000.0) ** (half / f32(DH))).astype(f32)
    t = np.arange(SEQ, dtype=f32)
    freqs = (t[:, None] * inv_freq[None, :]).astype(f32)
    freqs = np.concatenate([freqs, freqs], -1)
    base = ((half + f32(0.4 * DH)) / f32(1.4 * DH)).astype(f32)
    power = ((t - SEQ // 2) / f32(WIN // 2)).astype(f32)
    scale = (base[None, :] ** power[:, None]).astype(f32)
    scale = np.concatenate([scale, scale], -1)
    cos, sin = np.cos(freqs).astype(f32), np.sin(freqs).astype(f32)
    sin[:, :DH // 2] *= -1
    inv = f32(1.0) / scale
    rot = np.stack([cos * scale * 8, sin * scale * 8, cos * inv, sin * inv], 0).astype(f32)
    rot = rot.reshape(4, TPB, P, DH).transpose(2, 0, 1, 3)
    return {"c_ident": ident, "c_causal": causal, "c_wmask": wmask, "c_notfirst": notfirst, "c_rot": rot}


def layout(i):
    T = lambda a: a.T
    swap = lambda a: np.concatenate([a[:, DH // 2:], a[:, :DH // 2]], 1)
    rep = lambda a: np.broadcast_to(a[..., None, :], a.shape[:-1] + (P,) + a.shape[-1:])

    def ffn(w1, w2, b1, b2):
        return np.concatenate([w1.T, w2.T.reshape(4, P, DIM).transpose(1, 0, 2).reshape(P, FF),
                               b1.reshape(4, P).T, b2[:, None]], 1)

    def pieces(v):
        out = np.zeros((DEPTH, P, 3), v.dtype)
        for k in range(3):
            piece = v[:, k * P:(k + 1) * P]
            out[:, :piece.shape[1], k] = piece
        return out

    w2 = np.zeros((DEPTH, 3 * P, DIM), np.float32)
    w2[:, :DI] = i["L1_ffn_W2"]
    b1 = i["L1_ffn_b1"]
    qs, ks = i["L1_ffn_q_scale"], i["L1_ffn_k_scale"]
    experts = np.stack([ffn(i["L0_ffn_TW1"][e], i["L0_ffn_TW2"][e], i["L0_ffn_Tb1"][e], i["L0_ffn_Tb2"][e])
                        for e in range(EXPERTS)], 1)
    return {
        "x": T(i["L0_attn_x"].reshape(TOKENS, DIM)),
        "qkv_down": T(i["L0_attn_W_qkv_v"]), "qkv_up": T(i["L0_attn_W_qkv_u"]),
        "o_down": T(i["L0_attn_W_o_v"]), "o_up": T(i["L0_attn_W_o_u"]),
        "gate_w1": T(i["L0_ffn_gate_w1"]), "gate_b1": i["L0_ffn_gate_b1"][:, None],
        "gate_w2": T(i["L0_ffn_gate_w2"]), "gate_b2": rep(i["L0_ffn_gate_b2"]),
        "ffn_base": ffn(i["L0_ffn_W1"], i["L0_ffn_W2"], i["L0_ffn_b1"], i["L0_ffn_b2"]),
        "ffn_experts": experts,
        "wq": i["L1_attn_Wq"], "wk": i["L1_attn_Wk"], "wv": i["L1_attn_Wv"],
        "w_qkv": i["L1_ffn_Wqkv"],
        "w_scales": rep(np.stack([qs, swap(qs), ks, swap(ks)], 1).reshape(DEPTH, 4 * DH)).reshape(DEPTH, P, 4, DH),
        "w_o": i["L1_ffn_Wo"].reshape(DEPTH, INNER // P, P, DIM).transpose(0, 2, 1, 3),
        "w_1": i["L1_ffn_W1"],
        "w_2": w2.reshape(DEPTH, 3, P, DIM).transpose(0, 2, 1, 3),
        "w_vecs": np.concatenate([i["L1_ffn_ln_g"][:, :, None], i["L1_ffn_ln_b"][:, :, None],
                                  i["L1_ffn_b2"][:, :, None], np.zeros((DEPTH, P, 1), np.float32),
                                  pieces(b1[:, :DI]), pieces(b1[:, DI:])], 2),
    }


def kernel(**inputs):
    import concourse.bacc as _bacc
    from concourse.bass_utils import run_bass_kernel_spmd as _run

    nc = _bacc.Bacc("TRN2", target_bir_lowering=False, num_devices=1)
    arrays = {f"in_{k}": np.ascontiguousarray(v)
              for k, v in {**layout({k: np.asarray(v) for k, v in inputs.items()}), **shape_constants()}.items()}
    A = {k[3:]: nc.dram_tensor(k, v.shape, mybir.dt.from_np(v.dtype), kind="ExternalInput").ap()
         for k, v in arrays.items()}
    out = nc.dram_tensor("out_dram", (DIM, TOKENS), F32, kind="ExternalOutput").ap()
    build(nc, A, out)
    r = _run(nc, [arrays], core_ids=[0])
    return np.ascontiguousarray(r.results[0]["out_dram"].T).reshape(BATCH, SEQ, DIM)
```
